# Optimizing a Trainium2 kernel written in Bass

```python
import numpy as np
import jax
import jax.numpy as jnp

def _softmax(x, axis=-1):
    return jax.nn.softmax(x, axis=axis)

def _gelu(x):
    return jax.nn.gelu(x, approximate=True)

def _silu(x):
    return jax.nn.silu(x)

def _sigmoid(x):
    return jax.nn.sigmoid(x)

def _layernorm(x, axis=-1, eps=1e-05):
    m = jnp.mean(x, axis=axis, keepdims=True)
    v = jnp.var(x, axis=axis, keepdims=True)
    return (x - m) / jnp.sqrt(v + eps)

def _scatter_add(tgt, idx, src, axis=0):
    return tgt.at[idx].add(src)

def _segment_sum(src, seg, n):
    return jax.ops.segment_sum(src, seg, n)
kernel_name = 'mk_sandwich_d1_jaxref_r8_332a55'

def setup_inputs(seed: int=0):
    np.random.seed(seed)
    _w = jnp.asarray

    def _L0_attn_setup():
        import jax, jax.numpy as jnp
        import numpy as np
        B, L, H, N2 = (8, 256, 128, 32)

        def s4_kernel(log_dt, C_re, C_im, log_A_re, A_im, L):
            dt = jnp.exp(log_dt)
            C = C_re + 1j * C_im
            A = -jnp.exp(log_A_re) + 1j * A_im
            dtA = A * dt[:, None]
            Ck = C * (jnp.exp(dtA) - 1.0) / A
            K = jnp.exp(dtA[:, :, None] * jnp.arange(L, dtype=jnp.float32))
            return 2.0 * jnp.einsum('hn,hnl->hl', Ck, K).real
        key = jax.random.key(seed)
        ks = jax.random.split(key, 8)
        return {'x': jax.random.normal(ks[0], (B, L, H), dtype=jnp.float32), 'log_dt': jax.random.uniform(ks[1], (H,), dtype=jnp.float32) * (np.log(0.1) - np.log(0.001)) + np.log(0.001), 'C_re': jax.random.normal(ks[2], (H, N2), dtype=jnp.float32), 'C_im': jax.random.normal(ks[3], (H, N2), dtype=jnp.float32), 'log_A_re': jax.random.normal(ks[4], (H, N2), dtype=jnp.float32), 'A_im': jnp.ones((H, N2), dtype=jnp.float32), 'D': jax.random.normal(ks[5], (H,), dtype=jnp.float32), 'W': jax.random.normal(ks[6], (2 * H, H), dtype=jnp.float32) * (1.0 / np.sqrt(H)), 'b': jax.random.normal(ks[7], (2 * H,), dtype=jnp.float32) * 0.01}
    _L0_attn_in = _L0_attn_setup()

    def _L0_ffn_setup():
        import jax, jax.numpy as jnp
        import numpy as np
        DIM = 128
        HIDDEN = 384
        SCALE = 1.0 / 127.0

        def _dequant(w_int, dtype):
            return w_int.astype(dtype) * jnp.asarray(SCALE, dtype)
        key = jax.random.key(seed)
        k_x, k_g, k_u, k_d = jax.random.split(key, 4)
        x = jax.random.normal(k_x, (4, 256, DIM), dtype=jnp.float32)
        w_gate = jax.random.randint(k_g, (HIDDEN, DIM), -127, 128, dtype=jnp.int32)
        w_up = jax.random.randint(k_u, (HIDDEN, DIM), -127, 128, dtype=jnp.int32)
        w_down = jax.random.randint(k_d, (DIM, HIDDEN), -127, 128, dtype=jnp.int32)
        return {'x': x, 'w_gate': w_gate, 'w_up': w_up, 'w_down': w_down}
    _L0_ffn_in = _L0_ffn_setup()
    _d = {'L0_attn_x': _L0_attn_in['x'], 'L0_attn_log_dt': _L0_attn_in['log_dt'], 'L0_attn_C_re': _L0_attn_in['C_re'], 'L0_attn_C_im': _L0_attn_in['C_im'], 'L0_attn_log_A_re': _L0_attn_in['log_A_re'], 'L0_attn_A_im': _L0_attn_in['A_im'], 'L0_attn_D': _L0_attn_in['D'], 'L0_attn_W': _L0_attn_in['W'], 'L0_attn_b': _L0_attn_in['b'], 'L0_ffn_w_gate': _L0_ffn_in['w_gate'], 'L0_ffn_w_up': _L0_ffn_in['w_up'], 'L0_ffn_w_down': _L0_ffn_in['w_down']}
    _x0 = _d['L0_attn_x']
    _d['L0_attn_x'] = jax.random.normal(jax.random.fold_in(jax.random.key(seed), 1), (8, 512, 128), dtype=_x0.dtype)
    del _x0
    return _d

def reference(L0_attn_x, L0_attn_log_dt, L0_attn_C_re, L0_attn_C_im, L0_attn_log_A_re, L0_attn_A_im, L0_attn_D, L0_attn_W, L0_attn_b, L0_ffn_w_gate, L0_ffn_w_up, L0_ffn_w_down):

    def _L0_attn_ref(x, log_dt, C_re, C_im, log_A_re, A_im, D, W, b):
        import jax, jax.numpy as jnp
        import numpy as np
        B, L, H, N2 = (8, 256, 128, 32)

        def s4_kernel(log_dt, C_re, C_im, log_A_re, A_im, L):
            dt = jnp.exp(log_dt)
            C = C_re + 1j * C_im
            A = -jnp.exp(log_A_re) + 1j * A_im
            dtA = A * dt[:, None]
            Ck = C * (jnp.exp(dtA) - 1.0) / A
            K = jnp.exp(dtA[:, :, None] * jnp.arange(L, dtype=jnp.float32))
            return 2.0 * jnp.einsum('hn,hnl->hl', Ck, K).real
        Lx = x.shape[1]
        k = s4_kernel(log_dt, C_re, C_im, log_A_re, A_im, Lx)
        xt = jnp.transpose(x, (0, 2, 1))
        n = 2 * Lx
        y = jnp.fft.irfft(jnp.fft.rfft(xt, n=n) * jnp.fft.rfft(k, n=n), n=n)[..., :Lx]
        y = y + xt * D[:, None]
        y = jax.nn.gelu(y, approximate=False)
        z = jnp.einsum('oh,bhl->bol', W, y) + b[None, :, None]
        a, g = jnp.split(z, 2, axis=1)
        y = a * jax.nn.sigmoid(g)
        return jnp.transpose(y, (0, 2, 1)) + x

    def _L0_ffn_ref(x, w_gate, w_up, w_down):
        import jax, jax.numpy as jnp
        import numpy as np
        DIM = 128
        HIDDEN = 384
        SCALE = 1.0 / 127.0

        def _dequant(w_int, dtype):
            return w_int.astype(dtype) * jnp.asarray(SCALE, dtype)
        wg = _dequant(w_gate, x.dtype)
        wu = _dequant(w_up, x.dtype)
        wd = _dequant(w_down, x.dtype)
        gate = jnp.einsum('bsd,hd->bsh', x, wg)
        up = jnp.einsum('bsd,hd->bsh', x, wu)
        h = jax.nn.silu(gate) * up
        return jnp.einsum('bsh,dh->bsd', h, wd)
    x = L0_attn_x
    x = x + _layernorm(_L0_attn_ref(_layernorm(x, axis=-1), L0_attn_log_dt, L0_attn_C_re, L0_attn_C_im, L0_attn_log_A_re, L0_attn_A_im, L0_attn_D, L0_attn_W, L0_attn_b), axis=-1)
    x = x + _layernorm(_L0_ffn_ref(_layernorm(x, axis=-1), L0_ffn_w_gate, L0_ffn_w_up, L0_ffn_w_down), axis=-1)
    return x

_drawn_inputs = setup_inputs


def setup_inputs(seed=0):
    import zlib

    import numpy as np

    out = dict(_drawn_inputs(seed))
    spreads = {'L0_attn_A_im': (1.0, 0.2)}
    factors = {'L0_attn_b': 8.0}
    for name, (base, spread) in spreads.items():
        noise = np.random.default_rng([zlib.crc32(name.encode()), seed]).standard_normal(out[name].shape)
        drawn = base * np.exp(spread * noise) if base else spread * noise
        out[name] = jnp.asarray(drawn.astype(out[name].dtype))
    for name, factor in factors.items():
        out[name] = (out[name] * factor).astype(out[name].dtype)
    return out
```

```python
from contextlib import ExitStack

import numpy as np

import concourse.bass as bass
from concourse import mybir

B, L, H, N2 = 8, 512, 128, 32
HID = 384
P = 128
M = L // 2
MT = M // P
F = L
FT = F // P
T = L // P
J = HID // P
HQ = H // 2
NR = 32
NA = L // NR
NANG = NR + 2 * NA + 2
NMAG = NR + NA + 1
EPS = 1e-5
SCALE = 1.0 / 127.0
ROUND = 1.5 * 2.0**23
TWO_PI = 6.283185
UNIT = T * H

F32 = mybir.dt.float32
BF16 = mybir.dt.bfloat16
I32 = mybir.dt.int32
ALU = mybir.AluOpType
ACT = mybir.ActivationFunctionType


def shape_constants():
    m, f = np.arange(M), np.arange(F)
    angle = np.pi * np.outer(2 * m + 1, 2 * f + 1) / (4.0 * L)
    trig = np.stack([np.cos(angle), np.sin(angle)])
    fwd = trig.reshape(2, MT, P, F).transpose(2, 0, 1, 3).reshape(P, -1)
    inv = trig.transpose(0, 2, 1).reshape(2, FT, P, M).transpose(2, 0, 1, 3).reshape(P, -1)
    turn = np.pi * (2 * f + 1) * (L - 1) / (4.0 * L)
    c0, s0 = np.cos(turn) / L, np.sin(turn) / L
    rot = np.stack([c0, s0, -s0]).reshape(3, FT, P).transpose(2, 0, 1).reshape(P, -1)
    r, a = np.arange(NR), NR * np.arange(NA)
    powers = np.concatenate([r, a, a, [1, 1], r, a, [1]])
    is_re = (np.arange(P) // N2) % 2 == 0
    phase = np.zeros((P, NANG))
    phase[:, :NR] = np.where(is_re, 0.25, 0.0)[:, None]
    phase[:, NR:NR + NA] = 0.25
    phase[:, NR + 2 * NA] = 0.25
    re, im = is_re[:, None] * 2.0, ~is_re[:, None] * 2.0
    gen = np.concatenate([np.tile(powers, (P, 1)), phase, re, -im, -re, -im], axis=1)
    out = {"fwd": fwd, "inv": inv, "rot": rot, "gen": gen, "ident": np.eye(P), "parts3": np.eye(3)}
    return {k: np.ascontiguousarray(v, dtype=np.float32) for k, v in out.items()}


def build(nc, d):
    es = ExitStack()
    with es:
        def sb(name, shape, dt=F32):
            return es.enter_context(nc.sbuf_tensor(name, shape, dt))

        def sem(name):
            return es.enter_context(nc.semaphore(name))

        x_tok = sb("x_tok", [P, B, T, H])
        u_tok = sb("u_tok", [P, B, T, H])
        fold = sb("fold", [P, 2, MT, B, H])
        spec = sb("spec", [P, 2, FT, B, H])
        fwd = sb("fwd", [P, 2, MT, F])
        inv = sb("inv", [P, 2, FT, M])
        rot = sb("rot", [P, 3, FT])
        gen = sb("gen", [P, NANG + NMAG + NANG + 4])
        ident = sb("ident", [P, P])
        ssm = sb("ssm", [P, 5, HQ])
        d_col = sb("d_col", [P, 1])
        w_out = sb("w_out", [H, 2 * H])
        bias3 = sb("bias3", [3, 2 * H])
        parts3 = sb("parts3", [3, 3])
        bias_b = sb("bias_b", [3, 3, 2 * H], BF16)
        ones3 = sb("ones3", [3, P], BF16)
        w_int = sb("w_int", [P, 3 * HID], I32)
        w_ffn = sb("w_ffn", [P, 3 * HID])
        half_neg = sb("half_neg", [P, 2 * T])
        eps_t = sb("eps_t", [P, 2 * T])
        held = sb("held", [P, 1])
        small = sb("small", [P, 20, HQ])
        kspec = sb("kspec", [P, 2, FT, H])
        kh = sb("kh", [P, L])
        shared_d = sb("shared_d", [P, 4 * UNIT])
        k2s = shared_d[0:NR, :]
        kfold = sb("kfold", [P, 2, M])
        kfold_t = sb("kfold_t", [P, 2, MT, H])
        shared_a = sb("shared_a", [P, HQ * NMAG])
        magb = shared_a[:].rearrange("p (h k) -> p h k", h=HQ)
        shared_b = sb("shared_b", [P, HQ * NANG])
        angb = shared_b[:].rearrange("p (h k) -> p h k", h=HQ)
        shared = sb("shared", [P, HQ * NANG])
        rndb = shared[:].rearrange("p (h k) -> p h k", h=HQ)
        shared_c = sb("shared_c", [P, 3 * HQ * NR])
        bmat, umat, pmat = (shared_c[:, HQ * NR * k:HQ * NR * (k + 1)] for k in range(3))
        bmat = bmat.rearrange("p (h r) -> p h r", h=HQ)
        umat = umat.rearrange("p (v h a) -> p v h a", v=2, h=HQ)
        pmat = pmat.rearrange("p (h k) -> p h k", h=HQ)
        yspec = shared_b[:, 0:4 * UNIT].rearrange("p (s c f h) -> p s c f h", s=2, c=2, f=FT)
        term = shared_b[:, 4 * UNIT:8 * UNIT].rearrange("p (s c f h) -> p s c f h", s=2, c=2, f=FT)
        rot_t = shared_d[:, 0:2 * UNIT].rearrange("p (c f h) -> p c f h", c=2, f=FT)
        term_p = shared_d[:, 2 * UNIT:4 * UNIT].rearrange("p (c f h) -> p c f h", c=2, f=FT)
        odd = shared_c[:, 8 * UNIT:8 * UNIT + 2 * M].rearrange("p (s m) -> p s m", s=2)
        ypre = shared_a[:, 0:2 * L].rearrange("p (s l) -> p s l", s=2)
        yact = shared_a[:, 2 * L:4 * L].rearrange("p (s l) -> p s l", s=2)
        th = shared_a[:, 4 * L:4 * L + 2 * UNIT].rearrange("p (s t h) -> p s t h", s=2, t=T)
        tbuf = shared_c[:, 6 * UNIT:6 * UNIT + 2 * UNIT].rearrange("p (s t h) -> p s t h", s=2, t=T)
        st = sb("st", [P, 2, 2 * T, 6])
        mv = sb("mv", [P, 2, 2 * T, 2])
        rs = sb("rs", [P, 2, 2 * T])
        st3 = sb("st3", [P, 2, T, 6])
        mv3 = sb("mv3", [P, 2, T, 2])
        rs3 = sb("rs3", [P, 2, T])
        vbuf = shared_c[:, 0 * UNIT:0 * UNIT + 2 * UNIT].rearrange("p (s t h) -> p s t h", s=2, t=T)
        vt = shared_c[:, 2 * UNIT:2 * UNIT + 2 * UNIT].rearrange("p (s l) -> p s l", s=2)
        sg = shared_c[:, 4 * UNIT:4 * UNIT + 2 * UNIT].rearrange("p (s l) -> p s l", s=2)
        bias_w = shared[0:3, 6 * UNIT:8 * UNIT].rearrange("p (k o) -> p k o", k=4)
        hb = shared[:, 0:2 * J * L].rearrange("p (s j l) -> p s j l", s=2, j=J)

        bank = [es.enter_context(nc.psum_tensor(f"bank{i}", [P, 512], F32)) for i in range(8)]
        k_dram = d["k_scratch"]

        ssm_in, gen_in, fwd_in, inv_in, misc_in, ffn_in = map(
            sem, ("ssm_in", "gen_in", "fwd_in", "inv_in", "misc_in", "ffn_in"))
        x_in = [sem("x_in0"), sem("x_in1")]
        setup_p, bias_step, bias_ready, w_half, ffn_w = map(
            sem, ("setup_p", "bias_step", "bias_ready", "w_half", "ffn_w"))
        g_exp, g_rate, g_arg, g_mag, g_ang, g_sin, g_sm, g_ck, g_b, g_u, g_p, g_zero = map(
            sem, ("g_exp", "g_rate", "g_arg", "g_mag", "g_ang", "g_sin", "g_sm", "g_ck", "g_b",
                  "g_u", "g_p", "g_zero"))
        k2_done, k2_out, k_stored, k_back, kd_added, k_folded, kt_done, kt_out, kf_done, kr_half, k_ready = map(
            sem, ("k2_done", "k2_out", "k_stored", "k_back", "kd_added", "k_folded", "kt_done", "kt_out",
                  "kf_done", "kr_half", "k_ready"))
        ln1_bn, ln1_mv, ln1_var, ln1_rs, u_ready, fold_ready, fwd_done, fwd_out = map(
            sem, ("ln1_bn", "ln1_mv", "ln1_var", "ln1_rs", "u_ready", "fold_ready", "fwd_done", "fwd_out"))
        terms, re_done, terms_p, im_done, eo_done, odd_out, y_done, gelu_done, z_done, tanh_done = map(
            sem, ("terms", "re_done", "terms_p", "im_done", "eo_done", "odd_out", "y_done", "gelu_done",
                  "z_done", "tanh_done"))
        t_done, tu_done, bn2, mv2, var2, rs2, w2_done, x1_done = map(
            sem, ("t_done", "tu_done", "bn2", "mv2", "var2", "rs2", "w2_done", "x1_done"))
        bn3, mv3_s, var3, rs3_s, v_done, vt_done, vt_out, gu_done, silu_done, h_done = map(
            sem, ("bn3", "mv3_s", "var3", "rs3_s", "v_done", "vt_done", "vt_out", "gu_done", "silu_done",
                  "h_done"))
        dn_done, bn4, mv4, var4, rs4, w4_done, o_done, stored = map(
            sem, ("dn_done", "bn4", "mv4", "var4", "rs4", "w4_done", "o_done", "stored"))

        powers_ang = gen[:, 0:NANG]
        powers_mag = gen[:, NANG:NANG + NMAG]
        phase = gen[:, NANG + NMAG:2 * NANG + NMAG]
        SG = 2 * NANG + NMAG

        def rows(ap, n):
            return ap.unsqueeze(1).to_broadcast([P, n, ap.shape[1]])

        def cols(ap, n):
            return ap.unsqueeze(2).to_broadcast([P, ap.shape[1], n])

        def seq(ap, b):
            return ap[:, bass.ds(b, 1), :, :].rearrange("p a t h -> p (a t) h")

        def unit_steps(eng, lo, hi, step):
            with eng.Fori(lo // 2, hi // 2) as k:
                step(2 * k, 0)
                step(2 * k + 1, 1)

        block = es.enter_context(nc.Block())

        @block.sync
        def _(sp):
            sp.dma_start(ssm[:], d["ssm"].rearrange("p (k h) -> p k h", k=5)).then_inc(ssm_in, 16)
            sp.dma_start(gen[:], d["gen"]).then_inc(gen_in, 16)
            xd = d["x"].rearrange("b (t p) h -> p b t h", p=P)
            for g in range(2):
                for b in range(4 * g, 4 * g + 4):
                    sp.dma_start(x_tok[:, b], xd[:, b]).then_inc(x_in[g], 16)
                if g == 0:
                    sp.dma_start(fwd[:], d["fwd"].rearrange("p (c t f) -> p c t f", c=2, t=MT)).then_inc(fwd_in, 16)
            sp.dma_start(ident[:], d["ident"]).then_inc(misc_in, 16)
            sp.dma_start(rot[:], d["rot"].rearrange("p (c t) -> p c t", c=3)).then_inc(misc_in, 16)
            sp.dma_start(d_col[:], d["d"]).then_inc(misc_in, 16)
            sp.dma_start(w_out[:], d["w"]).then_inc(misc_in, 16)
            sp.dma_start(bias3[:], d["b"]).then_inc(misc_in, 16)
            sp.dma_start(parts3[:], d["parts3"]).then_inc(misc_in, 16)
            sp.dma_start(inv[:], d["inv"].rearrange("p (c t m) -> p c t m", c=2, t=FT)).then_inc(inv_in, 16)
            sp.dma_start(w_int[:], d["ffn"]).then_inc(ffn_in, 16)
            sp.wait_ge(k2_out, 4)
            kd = k_dram.rearrange("(q h) (a r) -> q a h r", q=2, r=NR)
            for q in range(2):
                sp.dma_start(kd[q], k2s[NA * q:NA * q + NA, :].rearrange("a (h r) -> a h r", r=NR)).then_inc(k_stored, 16)
            sp.wait_ge(k_stored, 32)
            sp.dma_start(kh[:], k_dram).then_inc(k_back, 16)
            od = d["out"].rearrange("b (t p) h -> p b t h", p=P)
            with sp.Fori(0, B) as i:
                sp.wait_ge(o_done, i + 1)
                sp.dma_start(od[:, bass.ds(i, 1)], x_tok[:, bass.ds(i, 1)]).then_inc(stored, 16)
            sp.wait_ge(stored, 16 * B)

        @block.gpsimd
        def _(pool):
            tt = nc.gpsimd.tensor_tensor
            nc.gpsimd.memset(half_neg[:], -0.5).then_inc(setup_p, 1)
            nc.gpsimd.memset(eps_t[:], EPS).then_inc(setup_p, 1)
            nc.gpsimd.memset(ones3[:], 1.0).then_inc(setup_p, 1)
            nc.gpsimd.memset(pmat[:], 0.0).then_inc(g_zero, 1)

            def rstd(var, out, tmp_ready, n_tmp, done):
                tt(out, var, eps_t[:, 0:out.shape[1]], ALU.add).then_inc(tmp_ready, 1)
                pool.wait_ge(tmp_ready, n_tmp)
                tt(out, out, half_neg[:, 0:out.shape[1]], ALU.pow).then_inc(done, 1)

            pool.wait_ge(setup_p, 3)
            def ln1_pair(j):
                pool.wait_ge(ln1_mv, j + 1)
                rstd(mv[:, 0, :, 1], rs[:, 0, :], ln1_var, j + 1, ln1_rs)
                pool.wait_ge(u_ready, j + 1)
                for mt in range(MT):
                    for c, op in ((0, ALU.add), (1, ALU.subtract)):
                        last = tt(fold[:, c, mt, bass.ds(2 * j, 2), :],
                                  u_tok[:, bass.ds(2 * j, 2), MT + mt, :], u_tok[:, bass.ds(2 * j, 2), mt, :], op)
                last.then_inc(fold_ready, 1)
            with pool.Fori(0, 2) as j:
                ln1_pair(j)
            pool.wait_ge(g_mag, 1)
            pool.wait_ge(g_sin, 1)
            for v in range(2):
                tt(umat[:, v], magb[:, :, NR:NR + NA], angb[:, :, NR + NA * v:NR + NA * v + NA], ALU.mult).then_inc(g_u, 1)
            pool.wait_ge(g_ck, 2)
            for v in range(2):
                pool.wait_ge(g_u, v + 1)
                tt(umat[:, v], umat[:, v], cols(small[:, 18 + v, :], NA), ALU.mult).then_inc(g_u, 1)
            pool.wait_ge(g_u, 4)
            pool.wait_ge(g_zero, 1)
            for q in range(2):
                pp = slice(64 * q, 64 * q + 64)
                tt(pmat[pp, :, NA * q:NA * q + NA], umat[pp, 0], umat[pp, 1], ALU.add).then_inc(g_p, 1)
                pool.wait_ge(g_p, q + 1)
            with pool.Fori(2, 4) as j:
                ln1_pair(j)

            def product(i, s):
                pool.wait_ge(k_ready, 1)
                if not isinstance(i, int) or i >= 2:
                    pool.wait_ge(eo_done, i - 1)
                else:
                    pool.wait_ge(fwd_out, 16)
                if not isinstance(i, int) or i >= 1:
                    pool.wait_ge(im_done, i)
                tt(term_p[:, 0], spec[:, 0, :, bass.ds(i, 1), :].rearrange("p f a h -> p (f a) h"), kspec[:, 1], ALU.mult).then_inc(terms_p, 1)
                tt(term_p[:, 1], spec[:, 1, :, bass.ds(i, 1), :].rearrange("p f a h -> p (f a) h"), kspec[:, 0], ALU.mult).then_inc(terms_p, 1)
                pool.wait_ge(terms_p, 2 * i + 2)
                tt(yspec[:, s, 1], term_p[:, 0], term_p[:, 1], ALU.add).then_inc(im_done, 1)

            def add_u(i, s):
                pool.wait_ge(t_done, i + 1)
                tt(tbuf[:, s], tbuf[:, s], seq(u_tok, i), ALU.add).then_inc(tu_done, 1)

            def add_x(i, s):
                pool.wait_ge(w2_done, i + 1)
                tt(seq(x_tok, i), seq(x_tok, i), tbuf[:, s], ALU.add).then_inc(x1_done, 1)

            def rstd2(i, s):
                pool.wait_ge(mv2, i + 1)
                rstd(mv[:, s, 0:T, 1], rs[:, s, 0:T], var2, i + 1, rs2)

            def step(i, s, first=0, more=True):
                if more:
                    product(i + 2, s)
                if first < 1:
                    return
                add_u(i - 1, 1 - s)
                if first > 1:
                    add_x(i - 2, s)
                rstd2(i - 1, 1 - s)

            product(0, 0)
            product(1, 1)
            step(0, 0, 0)
            step(1, 1, 1)
            unit_steps(pool, 2, B - 2, lambda i, s: step(i, s, 2))
            step(B - 2, 0, 2, False)
            step(B - 1, 1, 2, False)
            add_u(B - 1, 1)
            add_x(B - 2, 0)
            rstd2(B - 1, 1)
            add_x(B - 1, 1)

            def rstd3(i, s):
                pool.wait_ge(mv3_s, i + 1)
                rstd(mv3[:, s, :, 1], rs3[:, s, :], var3, i + 1, rs3_s)

            def result(i, s):
                pool.wait_ge(mv4, i + 1)
                rstd(mv[:, s, 0:T, 1], rs[:, s, 0:T], var4, i + 1, rs4)
                pool.wait_ge(w4_done, i + 1)
                tt(seq(x_tok, i), seq(x_tok, i), tbuf[:, s], ALU.add).then_inc(o_done, 1)

            def ffn_step(i, s, prev=True, more=True):
                if more:
                    rstd3(i + 2, s)
                if prev:
                    result(i - 1, 1 - s)

            rstd3(0, 0)
            rstd3(1, 1)
            ffn_step(0, 0, prev=False)
            ffn_step(1, 1)
            unit_steps(pool, 2, B - 2, ffn_step)
            ffn_step(B - 2, 0, more=False)
            ffn_step(B - 1, 1, more=False)
            result(B - 1, 1)

        @block.scalar
        def _(act):
            a = nc.scalar.activation
            act.wait_ge(ssm_in, 16)
            a(small[:, 0], ssm[:, 0], ACT.Exp).then_inc(g_exp, 1)
            a(small[:, 1], ssm[:, 4], ACT.Exp).then_inc(g_exp, 1)
            act.wait_ge(g_arg, 1)
            a(magb[:], magb[:], ACT.Exp).then_inc(g_mag, 1)
            act.wait_ge(g_ang, 4)
            a(angb[:], angb[:], ACT.Sin, scale=TWO_PI).then_inc(g_sin, 1)

            def evacuate(g):
                for n in range(2 * FT):
                    ft, c = n // 2, n % 2
                    act.wait_ge(fwd_done, g * 2 * FT + n + 1)
                    a(spec[:, c, ft, bass.ds(4 * g, 4), :].rearrange("p b h -> p (b h)"), bank[n % 4][:],
                      ACT.Copy).then_inc(fwd_out, 1)
            evacuate(0)
            for n in range(4):
                act.wait_ge(k2_done, n + 1)
                a(k2s[:, 512 * n:512 * n + 512], bank[4 + n][0:NR, :], ACT.Copy).then_inc(k2_out, 1)
            evacuate(1)
            act.wait_ge(kt_done, 1)
            a(kfold_t[:].rearrange("p c t h -> p (c t h)"), bank[4][:], ACT.Copy).then_inc(kt_out, 1)
            act.wait_ge(misc_in, 96)
            a(w_out[:, 0:H], w_out[:, 0:H], ACT.Copy, scale=0.5).then_inc(w_half, 1)
            act.wait_ge(ffn_in, 16)
            a(w_ffn[:], w_int[:], ACT.Copy, scale=SCALE).then_inc(ffn_w, 1)

            def odd_copy(i, s):
                act.wait_ge(eo_done, i + 1)
                if not isinstance(i, int) or i >= 2:
                    act.wait_ge(y_done, i - 1)
                a(odd[:, s], bank[s][:, M:2 * M], ACT.Copy).then_inc(odd_out, 1)

            def gelu(i, s):
                act.wait_ge(y_done, i + 1)
                if not isinstance(i, int) or i >= 2:
                    act.wait_ge(z_done, i - 1)
                a(yact[:, s], ypre[:, s], ACT.Gelu).then_inc(gelu_done, 1)

            def tanh(i, s):
                act.wait_ge(z_done, i + 1)
                if not isinstance(i, int) or i >= 2:
                    act.wait_ge(t_done, i - 1)
                for k in range(2):
                    g = bank[2 + 2 * s + k][:].rearrange("p (t o) -> p t o", t=2)[:, :, H:2 * H]
                    last = a(th[:, s, 2 * k:2 * k + 2, :], g, ACT.Tanh, scale=0.5)
                last.then_inc(tanh_done, 1)

            def step(i, s):
                odd_copy(i, s)
                gelu(i, s)
                tanh(i - 1, 1 - s)

            odd_copy(0, 0)
            gelu(0, 0)
            step(1, 1)
            unit_steps(act, 2, B, step)
            tanh(B - 1, 1)

            def v_copy(i, s):
                act.wait_ge(vt_done, i + 1)
                if not isinstance(i, int) or i >= 2:
                    act.wait_ge(gu_done, J * i - J)
                a(vt[:, s], bank[6 + s][:], ACT.Copy).then_inc(vt_out, 1)

            def silu(i, s, j):
                n = J * i + j
                r = (J * s + j) % 2
                act.wait_ge(gu_done, n + 1)
                if not isinstance(i, int) or n >= 2:
                    act.wait_ge(h_done, n - 1)
                a(sg[:, r], bank[2 * r][:], ACT.Silu).then_inc(silu_done, 1)

            def ffn_step(i, s, more=True):
                silu(i, s, 0)
                if more:
                    v_copy(i + 1, 1 - s)
                silu(i, s, 1)
                silu(i, s, 2)

            v_copy(0, 0)
            ffn_step(0, 0)
            ffn_step(1, 1)
            unit_steps(act, 2, B - 2, ffn_step)
            ffn_step(B - 2, 0)
            ffn_step(B - 1, 1, more=False)

        @block.vector
        def _(dve):
            tt, ts, stt = nc.vector.tensor_tensor, nc.vector.tensor_scalar, nc.vector.scalar_tensor_tensor

            def ln1_pair(j):
                for k in range(2):
                    for t in range(T):
                        nc.vector.bn_stats(st[:, 0, T * k + t, :], x_tok[:, bass.ds(2 * j + k, 1), t, :]
                                           .rearrange("p a h -> p (a h)")).then_inc(ln1_bn, 1)
                dve.wait_ge(ln1_bn, 2 * T * j + 2 * T)
                nc.vector.memset(held[:], 0.0)
                for n in range(2 * T):
                    last = nc.vector.bn_aggr(mv[:, 0, n, :], st[:, 0, n, :])
                last.then_inc(ln1_mv, 1)
                dve.wait_ge(ln1_rs, j + 1)
                for k in range(2):
                    for t in range(T):
                        n = T * k + t
                        last = ts(u_tok[:, bass.ds(2 * j + k, 1), t, :].rearrange("p a h -> p (a h)"),
                                  x_tok[:, bass.ds(2 * j + k, 1), t, :].rearrange("p a h -> p (a h)"),
                                  mv[:, 0, n, 0:1], rs[:, 0, n:n + 1], ALU.subtract, ALU.mult)
                last.then_inc(u_ready, 1)

            dve.wait_ge(g_exp, 2)
            dve.wait_ge(gen_in, 16)
            stt(small[:, 2], small[:, 0], -1.0, small[:, 1], ALU.mult, ALU.mult).then_inc(g_rate, 1)
            stt(small[:, 3], ssm[:, 1], float(1 / (2 * np.pi)), small[:, 1], ALU.mult, ALU.mult).then_inc(g_rate, 1)
            dve.wait_ge(g_rate, 2)
            tt(magb[:], cols(small[:, 2, :], NMAG), rows(powers_mag, HQ), ALU.mult).then_inc(g_arg, 1)
            tt(angb[:], cols(small[:, 3, :], NANG), rows(powers_ang, HQ), ALU.mult).then_inc(g_ang, 1)
            dve.wait_ge(g_ang, 1)
            tt(angb[:], angb[:], rows(phase, HQ), ALU.add).then_inc(g_ang, 1)
            dve.wait_ge(g_ang, 2)
            ts(rndb[:], angb[:], ROUND, -ROUND, ALU.add, ALU.add).then_inc(g_ang, 1)
            dve.wait_ge(g_ang, 3)
            tt(angb[:], angb[:], rndb[:], ALU.subtract).then_inc(g_ang, 1)

            dve.wait_ge(x_in[0], 64)
            with dve.Fori(0, 2) as j:
                ln1_pair(j)

            count = [0]

            def s_op(ins):
                count[0] += 1
                ins.then_inc(g_sm, 1)
                dve.wait_ge(g_sm, count[0])

            er, cw, sw = magb[:, :, NMAG - 1], angb[:, :, NANG - 2], angb[:, :, NANG - 1]
            g_, w_, cr, ci = small[:, 0], ssm[:, 1], ssm[:, 2], ssm[:, 3]

            def sm(k):
                return small[:, k]
            dve.wait_ge(g_mag, 1)
            dve.wait_ge(g_sin, 1)
            tt(bmat[:], magb[:, :, 0:NR], angb[:, :, 0:NR], ALU.mult).then_inc(g_b, 1)
            s_op(tt(sm(4), er, cw, ALU.mult))
            s_op(tt(sm(5), er, sw, ALU.mult))
            s_op(ts(sm(4), sm(4), -1.0, None, ALU.add))
            s_op(tt(sm(6), cr, sm(4), ALU.mult))
            s_op(tt(sm(7), ci, sm(5), ALU.mult))
            s_op(tt(sm(8), cr, sm(5), ALU.mult))
            s_op(tt(sm(9), ci, sm(4), ALU.mult))
            s_op(tt(sm(10), sm(6), sm(7), ALU.subtract))
            s_op(tt(sm(11), sm(8), sm(9), ALU.add))
            s_op(tt(sm(6), g_, g_, ALU.mult))
            s_op(tt(sm(7), w_, w_, ALU.mult))
            s_op(tt(sm(6), sm(6), sm(7), ALU.add))
            s_op(nc.vector.reciprocal(sm(12), sm(6)))
            s_op(tt(sm(6), sm(10), g_, ALU.mult))
            s_op(tt(sm(7), sm(11), w_, ALU.mult))
            s_op(tt(sm(8), sm(10), w_, ALU.mult))
            s_op(tt(sm(9), sm(11), g_, ALU.mult))
            s_op(tt(sm(13), sm(7), sm(6), ALU.subtract))
            s_op(tt(sm(14), sm(8), sm(9), ALU.add))
            s_op(tt(sm(13), sm(13), sm(12), ALU.mult))
            s_op(stt(sm(14), sm(14), -1.0, sm(12), ALU.mult, ALU.mult))
            s_op(ts(sm(15), sm(13), gen[:, SG:SG + 1], None, ALU.mult))
            s_op(ts(sm(16), sm(14), gen[:, SG + 2:SG + 3], None, ALU.mult))
            stt(sm(18), sm(14), gen[:, SG + 1:SG + 2], sm(15), ALU.mult, ALU.add).then_inc(g_ck, 1)
            stt(sm(19), sm(13), gen[:, SG + 3:SG + 4], sm(16), ALU.mult, ALU.add).then_inc(g_ck, 1)

            dve.wait_ge(x_in[1], 64)
            with dve.Fori(2, 4) as j:
                ln1_pair(j)

            dve.wait_ge(misc_in, 96)
            bcount = [0]

            def b_op(ins):
                bcount[0] += 1
                ins.then_inc(bias_step, 1)
                dve.wait_ge(bias_step, bcount[0])
            b_op(ts(bias3[:, 0:H], bias3[:, 0:H], 0.5, None, ALU.mult))
            b_op(nc.vector.tensor_copy(bias_b[:, 0], bias3[:]))
            b_op(tt(bias_w[:, 0], bias3[:], bias_b[:, 0], ALU.subtract))
            b_op(nc.vector.tensor_copy(bias_b[:, 1], bias_w[:, 0]))
            b_op(tt(bias_w[:, 1], bias_w[:, 0], bias_b[:, 1], ALU.subtract))
            b_op(ts(bias_w[:, 2], bias3[:], parts3[:, 0:1], None, ALU.mult))
            b_op(stt(bias_w[:, 3], bias_w[:, 0], parts3[:, 1:2], bias_w[:, 2], ALU.mult, ALU.add))
            b_op(stt(bias_w[:, 2], bias_w[:, 1], parts3[:, 2:3], bias_w[:, 3], ALU.mult, ALU.add))
            nc.vector.tensor_copy(bias_b[:, 2], bias_w[:, 2]).then_inc(bias_ready, 1)

            dve.wait_ge(k_back, 16)
            tt(kh[:, 0:1], kh[:, 0:1], d_col[:], ALU.add).then_inc(kd_added, 1)
            dve.wait_ge(kd_added, 1)
            low = kh[:, M - 1::-1] if False else kh[:, 0:M][:, ::-1]
            tt(kfold[:, 0], kh[:, M:L], low, ALU.add).then_inc(k_folded, 1)
            tt(kfold[:, 1], kh[:, M:L], low, ALU.subtract).then_inc(k_folded, 1)
            dve.wait_ge(kf_done, 1)
            for ft in range(FT):
                kr, ks = bank[5][:, H * ft:H * ft + H], bank[6][:, H * ft:H * ft + H]
                ts(rot_t[:, 0, ft], kr, rot[:, 0, ft:ft + 1], None, ALU.mult).then_inc(kr_half, 1)
                ts(rot_t[:, 1, ft], kr, rot[:, 1, ft:ft + 1], None, ALU.mult).then_inc(kr_half, 1)
            dve.wait_ge(kr_half, 2 * FT)
            for ft in range(FT):
                ks = bank[6][:, H * ft:H * ft + H]
                stt(kspec[:, 0, ft], ks, rot[:, 2, ft:ft + 1], rot_t[:, 0, ft], ALU.mult, ALU.add)
                last = stt(kspec[:, 1, ft], ks, rot[:, 0, ft:ft + 1], rot_t[:, 1, ft], ALU.mult, ALU.add)
            last.then_inc(k_ready, 1)
            dve.wait_ge(k_ready, 1)
            dve.wait_ge(fwd_out, 16)

            def product(i, s):
                if not isinstance(i, int) or i >= 2:
                    dve.wait_ge(eo_done, i - 1)
                tt(term[:, s, 0], spec[:, 0, :, bass.ds(i, 1), :].rearrange("p f a h -> p (f a) h"), kspec[:, 0], ALU.mult).then_inc(terms, 1)
                tt(term[:, s, 1], spec[:, 1, :, bass.ds(i, 1), :].rearrange("p f a h -> p (f a) h"), kspec[:, 1], ALU.mult).then_inc(terms, 1)
                dve.wait_ge(terms, 2 * i + 2)
                tt(yspec[:, s, 0], term[:, s, 0], term[:, s, 1], ALU.subtract).then_inc(re_done, 1)

            def unfold(i, s):
                dve.wait_ge(odd_out, i + 1)
                if not isinstance(i, int) or i >= 2:
                    dve.wait_ge(gelu_done, i - 1)
                tt(ypre[:, s, M:L], bank[s][:, 0:M], odd[:, s], ALU.add)
                tt(ypre[:, s, 0:M], bank[s][:, 0:M], odd[:, s], ALU.subtract).then_inc(y_done, 1)

            def gated(i, s):
                dve.wait_ge(tanh_done, i + 1)
                if not isinstance(i, int) or i >= 2:
                    dve.wait_ge(x1_done, i - 1)
                for k in range(2):
                    a_ = bank[2 + 2 * s + k][:].rearrange("p (t o) -> p t o", t=2)[:, :, 0:H]
                    last = stt(tbuf[:, s, 2 * k:2 * k + 2, :], th[:, s, 2 * k:2 * k + 2, :], 1.0, a_, ALU.add, ALU.mult)
                last.then_inc(t_done, 1)

            def moments(i, src, st_, mv_, bn, done):
                for t in range(T):
                    nc.vector.bn_stats(st_[:, t, :], src(t)).then_inc(bn, 1)
                dve.wait_ge(bn, T * i + T)
                nc.vector.memset(held[:], 0.0)
                for t in range(T):
                    last = nc.vector.bn_aggr(mv_[:, t, :], st_[:, t, :])
                last.then_inc(done, 1)

            def normalise(src, dst, mv_, rs_, done):
                for t in range(T):
                    last = ts(dst(t), src(t), mv_[:, t, 0:1], rs_[:, t:t + 1], ALU.subtract, ALU.mult)
                last.then_inc(done, 1)

            def moments2(i, s):
                dve.wait_ge(tu_done, i + 1)
                moments(i, lambda t: tbuf[:, s, t], st[:, s, 0:T], mv[:, s, 0:T], bn2, mv2)

            def norm2(i, s):
                dve.wait_ge(rs2, i + 1)
                normalise(lambda t: tbuf[:, s, t], lambda t: tbuf[:, s, t], mv[:, s], rs[:, s], w2_done)

            def step(i, s, first=2, more=True):
                unfold(i, s)
                if more:
                    product(i + 2, s)
                if first >= 1:
                    gated(i - 1, 1 - s)
                    if first >= 2:
                        norm2(i - 2, s)
                    moments2(i - 1, 1 - s)

            product(0, 0)
            product(1, 1)
            step(0, 0, 0)
            step(1, 1, 1)
            unit_steps(dve, 2, B - 2, step)
            step(B - 2, 0, more=False)
            step(B - 1, 1, more=False)
            gated(B - 1, 1)
            norm2(B - 2, 0)
            moments2(B - 1, 1)
            norm2(B - 1, 1)

            def x1_tile(i, t):
                return x_tok[:, bass.ds(i, 1), t, :].rearrange("p a h -> p (a h)")

            def moments3(i, s):
                dve.wait_ge(x1_done, i + 1)
                moments(i, lambda t: x1_tile(i, t), st3[:, s], mv3[:, s], bn3, mv3_s)

            def norm3(i, s):
                dve.wait_ge(rs3_s, i + 1)
                if not isinstance(i, int) or i >= 2:
                    dve.wait_ge(vt_done, i - 1)
                normalise(lambda t: x1_tile(i, t), lambda t: vbuf[:, s, t], mv3[:, s], rs3[:, s], v_done)

            def hidden(i, s, j):
                n = J * i + j
                r = (J * s + j) % 2
                dve.wait_ge(silu_done, n + 1)
                if j == 0 and (not isinstance(i, int) or i >= 2):
                    dve.wait_ge(dn_done, i - 1)
                tt(hb[:, s, j], sg[:, r], bank[2 * r + 1][:], ALU.mult).then_inc(h_done, 1)

            def moments4(i, s):
                dve.wait_ge(dn_done, i + 1)
                moments(i, lambda t: bank[4 + s][:, H * t:H * t + H], st[:, s, 0:T], mv[:, s, 0:T], bn4, mv4)

            def norm4(i, s):
                dve.wait_ge(rs4, i + 1)
                if not isinstance(i, int) or i >= 2:
                    dve.wait_ge(o_done, i - 1)
                normalise(lambda t: bank[4 + s][:, H * t:H * t + H], lambda t: tbuf[:, s, t], mv[:, s], rs[:, s], w4_done)

            def ffn_step(i, s, prev=True, more=True):
                hidden(i, s, 0)
                if more:
                    moments3(i + 2, s)
                hidden(i, s, 1)
                if more:
                    norm3(i + 2, s)
                if prev:
                    moments4(i - 1, 1 - s)
                hidden(i, s, 2)
                if prev:
                    norm4(i - 1, 1 - s)

            moments3(0, 0)
            moments3(1, 1)
            norm3(0, 0)
            norm3(1, 1)
            ffn_step(0, 0, prev=False)
            ffn_step(1, 1)
            unit_steps(dve, 2, B - 2, ffn_step)
            ffn_step(B - 2, 0, more=False)
            ffn_step(B - 1, 1, more=False)
            moments4(B - 1, 1)
            norm4(B - 1, 1)

        @block.tensor
        def _(pe):
            mm = nc.tensor.matmul
            pe.wait_ge(fwd_in, 16)

            def forward(g):
                pe.wait_ge(fold_ready, 2 * g + 2)
                for n in range(2 * FT):
                    ft, c = n // 2, n % 2
                    if g or n >= 4:
                        pe.wait_ge(fwd_out, 2 * FT * g + n - 3)
                    for mt in range(MT):
                        last = mm(bank[n % 4][:], fwd[:, c, mt, P * ft:P * ft + P],
                                  fold[:, c, mt, 4 * g:4 * g + 4, :].rearrange("p b h -> p (b h)"),
                                  start=(mt == 0), stop=(mt == MT - 1))
                    last.then_inc(fwd_done, 1)
            forward(0)
            pe.wait_ge(g_b, 1)
            pe.wait_ge(g_p, 2)
            for h in range(HQ):
                last = mm(bank[4 + h // 16][0:2 * NA, NR * (h % 16):NR * (h % 16) + NR], pmat[:, h, :], bmat[:, h, :],
                          start=True, stop=True)
                if h % 16 == 15:
                    last.then_inc(k2_done, 1)
            forward(1)
            pe.wait_ge(misc_in, 96)
            pe.wait_ge(k_folded, 2)
            pe.wait_ge(k2_out, 4)
            for n in range(2 * MT):
                last = nc.tensor.transpose(bank[4][:, H * n:H * n + H], kfold[:, n // MT, P * (n % MT):P * (n % MT) + P], ident[:])
            last.then_inc(kt_done, 1)
            pe.wait_ge(kt_out, 1)
            for c in range(2):
                for ft in range(FT):
                    for mt in range(MT):
                        last = mm(bank[5 + c][:, H * ft:H * ft + H], fwd[:, c, mt, P * ft:P * ft + P], kfold_t[:, c, mt, :],
                                  start=(mt == 0), stop=(mt == MT - 1))
            last.then_inc(kf_done, 1)

            def inverse(i, s):
                pe.wait_ge(re_done, i + 1)
                pe.wait_ge(im_done, i + 1)
                if not isinstance(i, int) or i >= 2:
                    pe.wait_ge(y_done, i - 1)
                for c in range(2):
                    for ft in range(FT):
                        last = mm(bank[s][:, M * c:M * c + M], yspec[:, s, c, ft, :], inv[:, c, ft, :],
                                  start=(ft == 0), stop=(ft == FT - 1))
                last.then_inc(eo_done, 1)

            def linear(i, s):
                pe.wait_ge(gelu_done, i + 1)
                if not isinstance(i, int) or i >= 2:
                    pe.wait_ge(t_done, i - 1)
                for t in range(T):
                    o = bank[2 + 2 * s + t // 2][:, 2 * H * (t % 2):2 * H * (t % 2) + 2 * H]
                    mm(o, ones3[:], bias_b[:, 2], start=True, stop=False)
                    last = mm(o, yact[:, s, P * t:P * t + P], w_out[:], start=False, stop=True)
                last.then_inc(z_done, 1)

            pe.wait_ge(inv_in, 16)
            inverse(0, 0)
            pe.wait_ge(bias_ready, 1)
            pe.wait_ge(w_half, 1)
            pe.wait_ge(setup_p, 3)

            def step(i, s):
                inverse(i + 1, 1 - s)
                linear(i, s)
            step(0, 0)
            step(1, 1)
            unit_steps(pe, 2, B - 2, step)
            step(B - 2, 0)
            linear(B - 1, 1)

            def turn_v(i, s):
                pe.wait_ge(v_done, i + 1)
                if not isinstance(i, int) or i >= 2:
                    pe.wait_ge(vt_out, i - 1)
                for t in range(T):
                    last = nc.tensor.transpose(bank[6 + s][:, P * t:P * t + P], vbuf[:, s, t, :], ident[:])
                last.then_inc(vt_done, 1)

            def gate_up(i, s, j):
                n = J * i + j
                r = (J * s + j) % 2
                if j == 0:
                    pe.wait_ge(vt_out, i + 1)
                if not isinstance(i, int) or n >= 2:
                    pe.wait_ge(h_done, n - 1)
                for k in range(2):
                    last = mm(bank[2 * r + k][:], w_ffn[:, HID * k + P * j:HID * k + P * j + P], vt[:, s, :], start=True, stop=True)
                last.then_inc(gu_done, 1)

            def down(i, s):
                pe.wait_ge(h_done, J * i + J)
                if not isinstance(i, int) or i >= 2:
                    pe.wait_ge(w4_done, i - 1)
                for t in range(T):
                    for j in range(J):
                        last = mm(bank[4 + s][:, H * t:H * t + H], hb[:, s, j, P * t:P * t + P],
                                  w_ffn[:, 2 * HID + H * j:2 * HID + H * j + H], start=(j == 0), stop=(j == J - 1))
                last.then_inc(dn_done, 1)

            def ffn_step(i, s, prev=True, more=True):
                gate_up(i, s, 0)
                if more:
                    turn_v(i + 1, 1 - s)
                gate_up(i, s, 1)
                if prev:
                    down(i - 1, 1 - s)
                gate_up(i, s, 2)

            pe.wait_ge(ffn_w, 1)
            turn_v(0, 0)
            pe.wait_ge(t_done, B)
            ffn_step(0, 0, prev=False)
            ffn_step(1, 1)
            unit_steps(pe, 2, B - 2, ffn_step)
            ffn_step(B - 2, 0)
            ffn_step(B - 1, 1, more=False)
            down(B - 1, 1)


def kernel(L0_attn_x, L0_attn_log_dt, L0_attn_C_re, L0_attn_C_im, L0_attn_log_A_re, L0_attn_A_im, L0_attn_D,
           L0_attn_W, L0_attn_b, L0_ffn_w_gate, L0_ffn_w_up, L0_ffn_w_down):
    import concourse.bacc as bacc
    from concourse.bass_utils import run_bass_kernel_spmd

    def spread(p):
        q = np.asarray(p).reshape(2, HQ, N2).transpose(0, 2, 1)
        return np.stack([q, q], axis=1).reshape(P, HQ)

    x = np.asarray(L0_attn_x)
    log_dt = np.broadcast_to(np.asarray(L0_attn_log_dt)[:, None], (H, N2))
    arrays = {
        "x": np.concatenate([x[:, M - 1::-1], x[:, M:]], axis=1),
        "ssm": np.concatenate([spread(p) for p in (L0_attn_log_A_re, L0_attn_A_im, L0_attn_C_re, L0_attn_C_im, log_dt)], axis=1),
        "d": np.asarray(L0_attn_D)[:, None],
        "w": np.asarray(L0_attn_W).T,
        "b": np.broadcast_to(np.asarray(L0_attn_b)[None, :], (3, 2 * H)),
        "ffn": np.concatenate([np.asarray(L0_ffn_w_gate).T, np.asarray(L0_ffn_w_up).T,
                               np.asarray(L0_ffn_w_down).T.reshape(J, P, H).transpose(1, 0, 2).reshape(P, HID)], axis=1),
    }
    arrays.update(shape_constants())
    nc = bacc.Bacc("TRN2", target_bir_lowering=False, num_devices=1)
    arrays = {f"in_{k}": np.ascontiguousarray(v) for k, v in arrays.items()}
    d = {k[3:]: nc.dram_tensor(k, v.shape, mybir.dt.from_np(v.dtype), kind="ExternalInput").ap() for k, v in arrays.items()}
    d["k_scratch"] = nc.dram_tensor("k_scratch", (H, L), F32).ap()
    d["out"] = nc.dram_tensor("out", (B, L, H), F32, kind="ExternalOutput").ap()
    build(nc, d)
    got = run_bass_kernel_spmd(nc, [arrays], core_ids=[0]).results[0]["out"]
    return np.concatenate([got[:, M - 1::-1], got[:, M:]], axis=1)
```

```python
from contextlib import ExitStack

import numpy as np

import concourse.bass as bass
from concourse import mybir

B, L, H, N2 = 8, 512, 128, 32
HID = 384
P = 128
M = L // 2
MT = M // P
F = L
FT = F // P
T = L // P
J = HID // P
HQ = H // 2
NR = 32
NA = L // NR
NA1 = NA + 1
PAIR = 2
EPS = 1e-5
SCALE = 1.0 / 127.0
ROUND = 1.5 * 2.0**23
TWO_PI = 6.283185
UNIT = T * H

F32 = mybir.dt.float32
F32R = mybir.dt.float32r
BF16 = mybir.dt.bfloat16
I32 = mybir.dt.int32
ALU = mybir.AluOpType
ACT = mybir.ActivationFunctionType


def shape_constants():
    m, f = np.arange(M), np.arange(F)
    angle = np.pi * np.outer(2 * m + 1, 2 * f + 1) / (4.0 * L)
    trig = np.stack([np.cos(angle), np.sin(angle)])
    fwd = trig.reshape(2, MT, P, F).transpose(2, 0, 1, 3).reshape(P, -1)
    inv = trig.transpose(0, 2, 1).reshape(2, FT, P, M).transpose(2, 0, 1, 3).reshape(P, -1)
    turn = np.pi * (2 * f + 1) * (L - 1) / (4.0 * L)
    c0, s0 = np.cos(turn) / L, np.sin(turn) / L
    rot = np.stack([c0, s0, -s0]).reshape(3, FT, P).transpose(2, 0, 1).reshape(P, -1)
    powers = np.concatenate([NR * np.arange(NA), [1], np.arange(NR)])
    is_re = ((np.arange(P) // N2) % 2 == 0)[:, None]
    signs = [is_re * 2.0, is_re * -2.0, ~is_re * -2.0]
    gen = np.concatenate([np.tile(powers, (P, 1)), np.where(is_re, 0.25, 0.0), *signs, np.full((P, 1), np.pi / 2)], axis=1)
    out = {"fwd": fwd, "inv": inv, "rot": rot, "gen": gen, "ident": np.eye(P), "parts3": np.eye(3)}
    return {k: np.ascontiguousarray(v, dtype=np.float32) for k, v in out.items()}


def build(nc, d):
    es = ExitStack()
    with es:
        def sb(name, shape, dt=F32):
            return es.enter_context(nc.sbuf_tensor(name, shape, dt))

        def sem(name):
            return es.enter_context(nc.semaphore(name))

        x_tok = sb("x_tok", [P, B, T, H])
        u_tok = sb("u_tok", [P, B, T, H])
        fold = sb("fold", [P, 2, MT, B, H])
        spec = sb("spec", [P, 2, FT, B, H])
        kspec = sb("kspec", [P, 2, FT, H])
        fwd = sb("fwd", [P, 2, MT, F])
        inv = sb("inv", [P, 2, FT, M])
        rot = sb("rot", [P, 3, FT])
        gen = sb("gen", [P, NA1 + NR + 5])
        ident = sb("ident", [P, P])
        ssm = sb("ssm", [P, 5, HQ])
        d_col = sb("d_col", [HQ, 2])
        w_out = sb("w_out", [H, 2 * H])
        bias3 = sb("bias3", [3, 2 * H])
        parts3 = sb("parts3", [3, 3])
        bias_b = sb("bias_b", [3, 3, 2 * H], BF16)
        ones3 = sb("ones3", [3, P], BF16)
        w_int = sb("w_int", [P, 3 * HID], I32)
        w_ffn = sb("w_ffn", [P, 3 * HID])
        half_neg = sb("half_neg", [P, PAIR * T])
        eps_t = sb("eps_t", [P, PAIR * T])
        zero_t = sb("zero_t", [P, PAIR * T])
        held = sb("held", [P, 1])
        small = sb("small", [P, 19, HQ])
        st = sb("st", [P, 2, PAIR * T, 6])
        mv = sb("mv", [P, 2, PAIR * T, 2])
        rs = sb("rs", [P, 2, PAIR * T])
        nb = sb("nb", [P, 2, PAIR * T])
        st3 = sb("st3", [P, 2, T, 6])
        mv3 = sb("mv3", [P, 2, T, 2])
        rs3 = sb("rs3", [P, 2, T])
        nb3 = sb("nb3", [P, 2, T])
        vh = sb("vh", [P, 2, L], F32R)
        vl = sb("vl", [P, 2, L], F32R)
        wh = sb("wh", [P, 2 * HID], F32R)
        wl = sb("wl", [P, 2 * HID], F32R)

        GA, GB = HQ * NA1, HQ * NR
        pool_a = sb("pool_a", [P, 2 * GA + 2 * GA + GA])
        mag_a = pool_a[:, 0:GA].rearrange("p (h k) -> p h k", h=HQ)
        t_a = pool_a[:, GA:2 * GA]
        u_a = pool_a[:, GA:3 * GA].rearrange("p (v k) -> p v k", v=2)
        k_a = pool_a[:, 3 * GA:5 * GA].rearrange("p (v k) -> p v k", v=2)
        ypre = pool_a[:, 0:2 * L].rearrange("p (s l) -> p s l", s=2)
        yact = pool_a[:, 2 * L:4 * L].rearrange("p (s l) -> p s l", s=2)
        th = pool_a[:, 4 * L:6 * L].rearrange("p (s t h) -> p s t h", s=2, t=T)
        tbuf = pool_a[:, 6 * L:8 * L].rearrange("p (s t h) -> p s t h", s=2, t=T)
        odd = pool_a[:, 8 * L:9 * L].rearrange("p (s m) -> p s m", s=2)
        pool_b = sb("pool_b", [P, 3 * GB])
        mag_b, t_b, k_b = (pool_b[:, GB * k:GB * (k + 1)] for k in range(3))
        yspec = pool_b[:, 0:4 * UNIT].rearrange("p (s c f h) -> p s c f h", s=2, c=2, f=FT)
        term = pool_b[:, 4 * UNIT:8 * UNIT].rearrange("p (s c f h) -> p s c f h", s=2, c=2, f=FT)
        term_p = pool_b[:, 8 * UNIT:10 * UNIT].rearrange("p (c f h) -> p c f h", c=2, f=FT)
        bias_w = pool_b[0:3, 10 * UNIT:12 * UNIT].rearrange("p (k o) -> p k o", k=4)
        pool_c = sb("pool_c", [P, 3 * GB])
        b_mat = pool_c[:, 0:GB].rearrange("p (h r) -> p h r", h=HQ)
        p_mat = pool_c[:, GB:2 * GB].rearrange("p (h k) -> p h k", h=HQ)
        k2s = pool_c[0:2 * NA, 2 * GB:3 * GB].rearrange("p (h r) -> p h r", h=HQ)
        kq = pool_c[0:HQ, 0:2 * L]
        kfold = pool_c[0:HQ, 2 * L:4 * L].rearrange("p (c q m) -> p c q m", c=2, q=2)
        kfold_t = pool_c[:, 4 * L:5 * L].rearrange("p (c t h) -> p c t h", c=2, t=MT)
        vbuf = pool_c[:, 0:2 * UNIT].rearrange("p (s t h) -> p s t h", s=2, t=T)
        sg = pool_c[:, 2 * UNIT:4 * UNIT].rearrange("p (s l) -> p s l", s=2)
        hb = pool_c[:, 4 * UNIT:10 * UNIT].rearrange("p (s j l) -> p s j l", s=2, j=J)

        bank = [es.enter_context(nc.psum_tensor(f"bank{i}", [P, 512], F32)) for i in range(8)]

        ssm_in, gen_in, fwd_in, inv_in, misc_in, ffn_in, setup_p, bias_step = (sem(n) for n in "ssm_in gen_in fwd_in inv_in misc_in ffn_in setup_p bias_step".split())
        bias_ready, w_half, ffn_w, ffn_wh, ffn_wl, g_exp, g_rate, g_arg_a = (sem(n) for n in "bias_ready w_half ffn_w ffn_wh ffn_wl g_exp g_rate g_arg_a".split())
        g_arg_b, g_mag_a, g_mag_b, g_ta, g_tb, g_tb_phase, g_ua, g_ka = (sem(n) for n in "g_arg_b g_mag_a g_mag_b g_ta g_tb g_tb_phase g_ua g_ka".split())
        g_fa, g_kb, g_fb, g_sin_a, g_sin_b, g_uv, g_sm, g_recip = (sem(n) for n in "g_fa g_kb g_fb g_sin_a g_sin_b g_uv g_sm g_recip".split())
        g_ck, g_b, g_pp, g_zero, k2_done, k2_out, kq_done, kq_out = (sem(n) for n in "g_ck g_b g_pp g_zero k2_done k2_out kq_done kq_out".split())
        kd_added, k_folded, kt_done, kt_out, kf_done, kr_turned, k_ready, ln1_bn = (sem(n) for n in "kd_added k_folded kt_done kt_out kf_done kr_turned k_ready ln1_bn".split())
        ln1_mv, ln1_step, ln1_rs, u_ready, fold_ready, fold0_ready, fwd_done, fwd_out, terms = (sem(n) for n in "ln1_mv ln1_step ln1_rs u_ready fold_ready fold0_ready fwd_done fwd_out terms".split())
        re_done, terms_p, im_done, eo_done, odd_out, y_done, gelu_done, z_done = (sem(n) for n in "re_done terms_p im_done eo_done odd_out y_done gelu_done z_done".split())
        tanh_done, t_done, tu_done, bn2, mv2_s, step2, rs2, w2_done = (sem(n) for n in "tanh_done t_done tu_done bn2 mv2_s step2 rs2 w2_done".split())
        x1_done, bn3, mv3_s, step3, rs3_s, v_done, vt_done, vh_done = (sem(n) for n in "x1_done bn3 mv3_s step3 rs3_s v_done vt_done vh_done".split())
        vl_done, gu_done, silu_done, h_done, dn_done, bn4, mv4, step4 = (sem(n) for n in "vl_done gu_done silu_done h_done dn_done bn4 mv4 step4".split())
        rs4, w4_done, o_done, stored = (sem(n) for n in "rs4 w4_done o_done stored".split())
        x_in = [sem(f"x_in{j}") for j in range(B // PAIR)]

        pow_a, pow_b = gen[:, 0:NA1], gen[:, NA1:NA1 + NR]
        PH = NA1 + NR

        def rows(ap, n):
            return ap.unsqueeze(1).to_broadcast([P, n, ap.shape[1]])

        def cols(ap, n):
            return ap.unsqueeze(2).to_broadcast([P, ap.shape[1], n])

        def seq(ap, b):
            return ap[:, bass.ds(b, 1), :, :].rearrange("p a t h -> p (a t) h")

        def tile_of(ap, b, t):
            return ap[:, bass.ds(b, 1), t, :].rearrange("p a h -> p (a h)")

        def spectrum(c, b):
            return spec[:, c, :, bass.ds(b, 1), :].rearrange("p f a h -> p (f a) h")

        def fold_pair(tt, j, done):
            b = slice(PAIR * j, PAIR * j + PAIR)
            for mt in range(MT):
                for c, op in ((0, ALU.add), (1, ALU.subtract)):
                    last = tt(fold[:, c, mt, b, :], u_tok[:, b, MT + mt, :], u_tok[:, b, mt, :], op)
            last.then_inc(done, 1)

        def fwd_bank(j, ft):
            return ft if j < 3 else (5, 6, 4, 7)[ft]

        GATE_UP = ((0, 6), (1, 2))

        def turn_bank(i, s):
            return bank[7] if s else bank[6] if isinstance(i, int) and i == 0 else bank[3]

        def past(i, n):
            return not isinstance(i, int) or i >= n

        def unit_steps(eng, lo, hi, step):
            with eng.Fori(lo // 2, hi // 2) as k:
                step(2 * k, 0)
                step(2 * k + 1, 1)

        block = es.enter_context(nc.Block())

        @block.sync
        def _(sp):
            sp.dma_start(ssm[:], d["ssm"].rearrange("p (k h) -> p k h", k=5)).then_inc(ssm_in, 16)
            xd = d["x"].rearrange("b (t p) h -> p b t h", p=P)

            def load_x(j):
                for b in range(PAIR * j, PAIR * j + PAIR):
                    sp.dma_start(x_tok[:, b], xd[:, b]).then_inc(x_in[j], 16)
            load_x(0)
            sp.dma_start(gen[:], d["gen"]).then_inc(gen_in, 16)
            sp.dma_start(fwd[:], d["fwd"].rearrange("p (c t f) -> p c t f", c=2, t=MT)).then_inc(fwd_in, 16)
            load_x(1)
            sp.dma_start(bias3[:], d["b"]).then_inc(misc_in, 16)
            sp.dma_start(parts3[:], d["parts3"]).then_inc(misc_in, 16)
            sp.dma_start(ident[:], d["ident"]).then_inc(misc_in, 16)
            sp.dma_start(rot[:], d["rot"].rearrange("p (c t) -> p c t", c=3)).then_inc(misc_in, 16)
            sp.dma_start(d_col[:], d["d"]).then_inc(misc_in, 16)
            sp.dma_start(w_out[:], d["w"]).then_inc(misc_in, 16)
            load_x(2)
            sp.dma_start(w_int[:], d["ffn"]).then_inc(ffn_in, 16)
            load_x(3)
            sp.dma_start(inv[:], d["inv"].rearrange("p (c t m) -> p c t m", c=2, t=FT)).then_inc(inv_in, 16)
            od = d["out"].rearrange("b (t p) h -> p b t h", p=P)
            with sp.Fori(0, B) as i:
                sp.wait_ge(o_done, i + 1)
                sp.dma_start(od[:, bass.ds(i, 1)], x_tok[:, bass.ds(i, 1)]).then_inc(stored, 16)
            sp.wait_ge(stored, 16 * B)

        @block.gpsimd
        def _(pool):
            tt = nc.gpsimd.tensor_tensor
            nc.gpsimd.memset(half_neg[:], -0.5).then_inc(setup_p, 1)
            nc.gpsimd.memset(eps_t[:], EPS).then_inc(setup_p, 1)
            nc.gpsimd.memset(zero_t[:], 0.0).then_inc(setup_p, 1)
            nc.gpsimd.memset(ones3[:], 1.0).then_inc(setup_p, 1)
            nc.gpsimd.memset(p_mat, 0.0).then_inc(g_zero, 1)
            pool.wait_ge(setup_p, 4)

            def rstd(n, mean_var, rs_, nb_, step, done):
                k = rs_.shape[1]
                tt(rs_, mean_var[:, :, 1], eps_t[:, 0:k], ALU.add).then_inc(step, 1)
                pool.wait_ge(step, 3 * n + 1)
                tt(rs_, rs_, half_neg[:, 0:k], ALU.pow).then_inc(step, 1)
                pool.wait_ge(step, 3 * n + 2)
                tt(nb_, mean_var[:, :, 0], rs_, ALU.mult).then_inc(step, 1)
                pool.wait_ge(step, 3 * n + 3)
                tt(nb_, zero_t[:, 0:k], nb_, ALU.subtract).then_inc(done, 1)

            def ln1_rstd(j):
                pool.wait_ge(ln1_mv, j + 1)
                if j >= 2:
                    pool.wait_ge(u_ready, j - 1)
                rstd(j, mv[:, j % 2], rs[:, j % 2], nb[:, j % 2], ln1_step, ln1_rs)

            def ln1_fold(j):
                pool.wait_ge(u_ready, j + 1)
                fold_pair(nc.gpsimd.tensor_tensor, j, fold_ready)

            sm = [small[:, k] for k in range(19)]
            g_, w_, cr, ci = sm[0], ssm[:, 1], ssm[:, 2], ssm[:, 3]
            count = [0]

            def s_op(out, a, b, op):
                count[0] += 1
                tt(out, a, b, op).then_inc(g_sm, 1)

            def s_wait():
                pool.wait_ge(g_sm, count[0])

            pool.wait_ge(gen_in, 16)
            pool.wait_ge(g_rate, 2)
            tt(mag_b.rearrange("p (h r) -> p h r", h=HQ), cols(sm[2], NR), rows(pow_b, HQ), ALU.mult).then_inc(g_arg_b, 1)
            ln1_rstd(0)
            s_op(sm[6], g_, g_, ALU.mult)
            s_op(sm[7], w_, w_, ALU.mult)
            s_op(sm[8], cr, g_, ALU.mult)
            s_op(sm[9], ci, w_, ALU.mult)
            s_op(sm[10], cr, w_, ALU.mult)
            s_op(sm[11], ci, g_, ALU.mult)
            s_wait()
            s_op(sm[12], sm[6], sm[7], ALU.add)
            s_op(sm[14], sm[9], sm[8], ALU.subtract)
            s_op(sm[15], sm[10], sm[11], ALU.add)
            s_wait()
            ln1_rstd(1)
            pool.wait_ge(g_recip, 1)
            s_op(sm[14], sm[14], sm[13], ALU.mult)
            s_op(sm[15], sm[15], sm[13], ALU.mult)
            ln1_fold(1)
            pool.wait_ge(g_mag_a, 1)
            pool.wait_ge(g_sin_a, 2)
            er = mag_a[:, :, NA]
            sin_a = k_a.rearrange("p v (h k) -> p v h k", h=HQ)
            s_op(sm[4], er, sin_a[:, 1, :, NA], ALU.mult)
            s_op(sm[5], er, sin_a[:, 0, :, NA], ALU.mult)
            s_wait()
            nc.gpsimd.tensor_scalar(sm[4], sm[4], -1.0, None, ALU.add).then_inc(g_sm, 1)
            count[0] += 1
            s_wait()
            s_op(sm[6], sm[14], sm[4], ALU.mult)
            s_op(sm[7], sm[15], sm[5], ALU.mult)
            s_op(sm[8], sm[14], sm[5], ALU.mult)
            s_op(sm[9], sm[15], sm[4], ALU.mult)
            s_wait()
            tt(sm[16], sm[6], sm[7], ALU.add).then_inc(g_ck, 1)
            tt(sm[17], sm[8], sm[9], ALU.subtract).then_inc(g_ck, 1)
            ln1_rstd(2)
            pool.wait_ge(g_mag_b, 1)
            pool.wait_ge(g_sin_b, 1)
            tt(b_mat, mag_b.rearrange("p (h r) -> p h r", h=HQ), k_b.rearrange("p (h r) -> p h r", h=HQ), ALU.mult).then_inc(g_b, 1)
            ln1_fold(2)
            ln1_rstd(3)
            pool.wait_ge(ffn_w, 1)
            pool.wait_ge(ffn_wh, 1)
            tt(wl[:], w_ffn[:, 0:2 * HID], wh[:].bitcast(F32), ALU.subtract).then_inc(ffn_wl, 1)
            ln1_fold(3)

            def product(i, s):
                pool.wait_ge(k_ready, 2)
                if past(i, 2):
                    pool.wait_ge(eo_done, i - 1)
                else:
                    pool.wait_ge(fwd_out, FT)
                if past(i, 1):
                    pool.wait_ge(im_done, i)
                tt(term_p[:, 0], spectrum(0, i), kspec[:, 1], ALU.mult).then_inc(terms_p, 1)
                tt(term_p[:, 1], spectrum(1, i), kspec[:, 0], ALU.mult).then_inc(terms_p, 1)
                pool.wait_ge(terms_p, 2 * i + 2)
                tt(yspec[:, s, 1], term_p[:, 0], term_p[:, 1], ALU.add).then_inc(im_done, 1)

            def rstd2(i, s):
                pool.wait_ge(mv2_s, i + 1)
                rstd(i, mv[:, s, 0:T], rs[:, s, 0:T], nb[:, s, 0:T], step2, rs2)

            def rstd3(i, s):
                pool.wait_ge(mv3_s, i + 1)
                rstd(i, mv3[:, s], rs3[:, s], nb3[:, s], step3, rs3_s)

            def rstd4(i, s):
                pool.wait_ge(mv4, i + 1)
                rstd(i, mv[:, s, 0:T], rs[:, s, 0:T], nb[:, s, 0:T], step4, rs4)

            product(0, 0)
            product(1, 1)
            pool.wait_ge(fwd_out, 2 * FT)
            product(2, 0)

            def step(i, s):
                rstd2(i - 2, s)
                product(i + 2, s)
            product(3, 1)
            pool.wait_ge(fwd_out, FT * (B // PAIR))
            pool.wait_ge(u_ready, B // PAIR)
            unit_steps(pool, 2, B - 2, step)
            rstd3(0, 0)
            rstd3(1, 1)
            rstd2(B - 4, 0)
            rstd2(B - 3, 1)
            rstd2(B - 2, 0)
            rstd3(2, 0)
            rstd2(B - 1, 1)

            def ffn_step(i, s):
                rstd3(i + 2, s)
                rstd4(i - 1, 1 - s)
            ffn_step(1, 1)
            unit_steps(pool, 2, B - 2, ffn_step)
            rstd4(B - 3, 1)
            rstd4(B - 2, 0)
            rstd4(B - 1, 1)

        @block.scalar
        def _(act):
            a = nc.scalar.activation
            act.wait_ge(ssm_in, 16)
            a(small[:, 0], ssm[:, 0], ACT.Exp).then_inc(g_exp, 1)
            a(small[:, 1], ssm[:, 4], ACT.Exp).then_inc(g_exp, 1)
            act.wait_ge(g_arg_a, 1)
            a(mag_a, mag_a, ACT.Exp).then_inc(g_mag_a, 1)
            def normalise(src, dst, rs_, nb_, done):
                n = rs_.shape[1]
                for t in range(n):
                    last = a(dst(t), src(t), ACT.Identity, scale=rs_[:, t:t + 1], bias=nb_[:, t:t + 1])
                last.then_inc(done, 1)

            def ln1_norm(j):
                act.wait_ge(ln1_rs, j + 1)
                normalise(lambda n: tile_of(x_tok, PAIR * j + n // T, n % T), lambda n: tile_of(u_tok, PAIR * j + n // T, n % T),
                          rs[:, j % 2], nb[:, j % 2], u_ready)

            def evacuate(j, lo=0, hi=FT):
                for ft in range(lo, hi):
                    act.wait_ge(fwd_done, FT * j + ft + 1)
                    a(spec[:, :, ft, PAIR * j:PAIR * j + PAIR, :], bank[fwd_bank(j, ft)][:].rearrange("p (c b h) -> p c b h", c=2, b=PAIR),
                      ACT.Copy).then_inc(fwd_out, 1)

            ln1_norm(0)
            act.wait_ge(gen_in, 16)
            act.wait_ge(g_tb, 1)
            a(t_b, t_b, ACT.Identity, bias=gen[:, PH:PH + 1]).then_inc(g_tb_phase, 1)
            ln1_norm(1)
            act.wait_ge(g_arg_b, 1)
            a(mag_b, mag_b, ACT.Exp).then_inc(g_mag_b, 1)
            act.wait_ge(g_fa, 2)
            a(k_a[:, 0], k_a[:, 0], ACT.Sin, scale=TWO_PI).then_inc(g_sin_a, 1)
            a(k_a[:, 1], k_a[:, 1], ACT.Sin, scale=-TWO_PI, bias=gen[:, PH + 4:PH + 5]).then_inc(g_sin_a, 1)
            act.wait_ge(g_fb, 1)
            a(k_b, k_b, ACT.Sin, scale=TWO_PI).then_inc(g_sin_b, 1)
            evacuate(0)
            ln1_norm(2)
            act.wait_ge(misc_in, 96)
            a(w_out[:, 0:H], w_out[:, 0:H], ACT.Copy, scale=0.5).then_inc(w_half, 1)
            act.wait_ge(ffn_in, 16)
            a(w_ffn[:], w_int[:], ACT.Copy, scale=SCALE).then_inc(ffn_w, 1)
            act.wait_ge(ffn_w, 1)
            a(wh[:], w_ffn[:, 0:2 * HID], ACT.Copy).then_inc(ffn_wh, 1)
            evacuate(1)
            for n in range(2):
                act.wait_ge(k2_done, n + 1)
                a(k2s[:, 16 * n:16 * n + 16, :], bank[4 + n][0:2 * NA, :].rearrange("p (h r) -> p h r", h=16),
                  ACT.Copy).then_inc(k2_out, 1)
            ln1_norm(3)
            evacuate(2, 0, 2)
            act.wait_ge(kt_done, 1)
            a(kfold_t.rearrange("p c t h -> p (c t h)"), bank[6][:], ACT.Copy).then_inc(kt_out, 1)
            evacuate(2, 2, 4)
            evacuate(3, 0, 2)

            def odd_copy(i, s):
                act.wait_ge(eo_done, i + 1)
                if past(i, 2):
                    act.wait_ge(y_done, i - 1)
                a(odd[:, s], bank[s][:, M:2 * M], ACT.Copy).then_inc(odd_out, 1)

            def gelu(i, s):
                act.wait_ge(y_done, i + 1)
                if past(i, 2):
                    act.wait_ge(z_done, i - 1)
                a(yact[:, s], ypre[:, s], ACT.Gelu).then_inc(gelu_done, 1)

            def tanh(i, s):
                act.wait_ge(z_done, i + 1)
                if past(i, 2):
                    act.wait_ge(t_done, i - 1)
                for k in range(2):
                    g = bank[2 + 2 * s + k][:].rearrange("p (t o) -> p t o", t=2)[:, :, H:2 * H]
                    last = a(th[:, s, 2 * k:2 * k + 2, :], g, ACT.Tanh, scale=0.5)
                last.then_inc(tanh_done, 1)

            def norm2(i, s):
                act.wait_ge(rs2, i + 1)
                normalise(lambda t: tbuf[:, s, t], lambda t: tbuf[:, s, t], rs[:, s, 0:T], nb[:, s, 0:T], w2_done)

            def norm3(i, s):
                act.wait_ge(rs3_s, i + 1)
                if past(i, 2):
                    act.wait_ge(vt_done, i - 1)
                normalise(lambda t: tile_of(x_tok, i, t), lambda t: vbuf[:, s, t], rs3[:, s], nb3[:, s], v_done)

            def norm4(i, s):
                act.wait_ge(rs4, i + 1)
                normalise(lambda t: bank[4 + s][:, H * t:H * t + H], lambda t: tbuf[:, s, t], rs[:, s, 0:T], nb[:, s, 0:T], w4_done)

            def v_high(i, s):
                act.wait_ge(vt_done, i + 1)
                if past(i, 2):
                    act.wait_ge(gu_done, J * i - J)
                a(vh[:, s], turn_bank(i, s)[:], ACT.Copy).then_inc(vh_done, 1)

            def silu(i, s, j):
                n = J * i + j
                r = (J * s + j) % 2
                act.wait_ge(gu_done, n + 1)
                if past(n, 2):
                    act.wait_ge(h_done, n - 1)
                a(sg[:, r], bank[GATE_UP[r][0]][:], ACT.Silu).then_inc(silu_done, 1)

            def step(i, s, older=True):
                odd_copy(i, s)
                gelu(i, s)
                tanh(i - 1, 1 - s)
                if older:
                    norm2(i - 2, s)

            odd_copy(0, 0)
            gelu(0, 0)
            evacuate(3, 2, 4)
            step(1, 1, older=False)
            unit_steps(act, 2, B - 2, step)
            odd_copy(B - 2, 0)
            gelu(B - 2, 0)
            tanh(B - 3, 1)
            norm3(0, 0)
            odd_copy(B - 1, 1)
            gelu(B - 1, 1)
            v_high(0, 0)
            norm3(1, 1)
            tanh(B - 2, 0)
            norm2(B - 4, 0)
            tanh(B - 1, 1)
            silu(0, 0, 0)
            norm2(B - 3, 1)
            silu(0, 0, 1)
            v_high(1, 1)
            norm2(B - 2, 0)
            silu(0, 0, 2)
            norm3(2, 0)
            norm2(B - 1, 1)

            def ffn_step(i, s, older=True, more=2):
                silu(i, s, 0)
                silu(i, s, 1)
                if more >= 1:
                    v_high(i + 1, 1 - s)
                if older:
                    norm4(i - 2, s)
                if more >= 2:
                    norm3(i + 2, s)
                silu(i, s, 2)
            ffn_step(1, 1, older=False)
            unit_steps(act, 2, B - 2, ffn_step)
            ffn_step(B - 2, 0, more=1)
            ffn_step(B - 1, 1, more=0)
            norm4(B - 2, 0)
            norm4(B - 1, 1)

        @block.vector
        def _(dve):
            tt, ts, stt = nc.vector.tensor_tensor, nc.vector.tensor_scalar, nc.vector.scalar_tensor_tensor

            def moments(n, src, st_, mv_, bn, done):
                k = st_.shape[1]
                for t in range(k):
                    nc.vector.bn_stats(st_[:, t, :], src(t)).then_inc(bn, 1)
                dve.wait_ge(bn, n + k)
                nc.vector.memset(held[:], 0.0)
                for t in range(k):
                    last = nc.vector.bn_aggr(mv_[:, t, :], st_[:, t, :])
                last.then_inc(done, 1)

            def ln1_moments(j):
                dve.wait_ge(x_in[j], 16 * PAIR)
                if j >= 2:
                    dve.wait_ge(ln1_rs, j - 1)
                moments(PAIR * T * j, lambda n: tile_of(x_tok, PAIR * j + n // T, n % T), st[:, j % 2], mv[:, j % 2], ln1_bn, ln1_mv)

            dve.wait_ge(g_exp, 2)
            stt(small[:, 2], small[:, 0], -1.0, small[:, 1], ALU.mult, ALU.mult).then_inc(g_rate, 1)
            stt(small[:, 3], ssm[:, 1], float(1 / (2 * np.pi)), small[:, 1], ALU.mult, ALU.mult).then_inc(g_rate, 1)
            ln1_moments(0)
            dve.wait_ge(g_rate, 2)
            dve.wait_ge(gen_in, 16)
            tt(mag_a, cols(small[:, 2, :], NA1), rows(pow_a, HQ), ALU.mult).then_inc(g_arg_a, 1)
            tt(t_b.rearrange("p (h r) -> p h r", h=HQ), cols(small[:, 3, :], NR), rows(pow_b, HQ), ALU.mult).then_inc(g_tb, 1)
            ln1_moments(1)
            tt(t_a.rearrange("p (h k) -> p h k", h=HQ), cols(small[:, 3, :], NA1), rows(pow_a, HQ), ALU.mult).then_inc(g_ta, 1)
            dve.wait_ge(u_ready, 1)
            fold_pair(tt, 0, fold0_ready)
            dve.wait_ge(g_sm, 7)
            nc.vector.reciprocal(small[:, 13], small[:, 12]).then_inc(g_recip, 1)
            dve.wait_ge(g_ta, 1)
            ts(k_a[:, 1], t_a, ROUND, -ROUND, ALU.add, ALU.add).then_inc(g_ka, 1)
            dve.wait_ge(g_ka, 1)
            tt(k_a[:, 0], t_a, k_a[:, 1], ALU.subtract).then_inc(g_fa, 1)
            dve.wait_ge(g_fa, 1)
            stt(k_a[:, 1], k_a[:, 0], -1.0, k_a[:, 0], ALU.mult, ALU.max).then_inc(g_fa, 1)
            dve.wait_ge(g_tb_phase, 1)
            ts(k_b, t_b, ROUND, -ROUND, ALU.add, ALU.add).then_inc(g_kb, 1)
            dve.wait_ge(g_kb, 1)
            tt(k_b, t_b, k_b, ALU.subtract).then_inc(g_fb, 1)
            ln1_moments(2)
            dve.wait_ge(g_mag_a, 1)
            dve.wait_ge(g_sin_a, 2)
            sin_a = k_a.rearrange("p v (h k) -> p v h k", h=HQ)
            for v in range(2):
                tt(sin_a[:, v, :, 0:NA], mag_a[:, :, 0:NA], sin_a[:, v, :, 0:NA], ALU.mult).then_inc(g_uv, 1)
            dve.wait_ge(g_ck, 2)
            ts(small[:, 8], small[:, 16], gen[:, PH + 1:PH + 2], None, ALU.mult).then_inc(g_uv, 1)
            ts(small[:, 9], small[:, 16], gen[:, PH + 3:PH + 4], None, ALU.mult).then_inc(g_uv, 1)
            dve.wait_ge(g_uv, 4)
            stt(small[:, 10], small[:, 17], gen[:, PH + 3:PH + 4], small[:, 8], ALU.mult, ALU.add).then_inc(g_uv, 1)
            stt(small[:, 11], small[:, 17], gen[:, PH + 2:PH + 3], small[:, 9], ALU.mult, ALU.add).then_inc(g_uv, 1)
            dve.wait_ge(g_uv, 6)
            for v, c in ((1, 10), (0, 11)):
                tt(sin_a[:, v, :, 0:NA], sin_a[:, v, :, 0:NA], cols(small[:, c, :], NA), ALU.mult).then_inc(g_uv, 1)
            dve.wait_ge(g_uv, 8)
            dve.wait_ge(g_zero, 1)
            for q in range(2):
                pp = slice(64 * q, 64 * q + 64)
                tt(p_mat[pp, :, NA * q:NA * q + NA], sin_a[pp, 0, :, 0:NA], sin_a[pp, 1, :, 0:NA], ALU.add).then_inc(g_pp, 1)
            ln1_moments(3)

            dve.wait_ge(misc_in, 96)
            bcount = [0]

            def b_op(ins):
                bcount[0] += 1
                ins.then_inc(bias_step, 1)
                dve.wait_ge(bias_step, bcount[0])
            dve.wait_ge(g_b, 1)
            b_op(ts(bias3[:, 0:H], bias3[:, 0:H], 0.5, None, ALU.mult))
            b_op(nc.vector.tensor_copy(bias_b[:, 0], bias3[:]))
            b_op(tt(bias_w[:, 0], bias3[:], bias_b[:, 0], ALU.subtract))
            b_op(nc.vector.tensor_copy(bias_b[:, 1], bias_w[:, 0]))
            for n in range(2, 4):
                dve.wait_ge(k2_done, n + 1)
                nc.vector.tensor_copy(k2s[:, 16 * n:16 * n + 16, :],
                                      bank[4 + n][0:2 * NA, :].rearrange("p (h r) -> p h r", h=16)).then_inc(k2_out, 1)
            b_op(tt(bias_w[:, 1], bias_w[:, 0], bias_b[:, 1], ALU.subtract))
            b_op(ts(bias_w[:, 2], bias3[:], parts3[:, 0:1], None, ALU.mult))
            b_op(stt(bias_w[:, 3], bias_w[:, 0], parts3[:, 1:2], bias_w[:, 2], ALU.mult, ALU.add))
            b_op(stt(bias_w[:, 2], bias_w[:, 1], parts3[:, 2:3], bias_w[:, 3], ALU.mult, ALU.add))
            nc.vector.tensor_copy(bias_b[:, 2], bias_w[:, 2]).then_inc(bias_ready, 1)

            for n in range(2):
                dve.wait_ge(kq_done, n + 1)
                nc.vector.tensor_copy(kq[:, L * n:L * n + L], bank[4 + n][0:HQ, :]).then_inc(kq_out, 1)
            dve.wait_ge(kq_out, 2)
            kqv = kq.rearrange("p (r q a) -> p q a r", r=NR, q=2)
            tt(kq[:, 0:2 * NA:NA], kq[:, 0:2 * NA:NA], d_col[:], ALU.add).then_inc(kd_added, 1)
            dve.wait_ge(kd_added, 1)
            for q in range(2):
                high = kqv[:, q, NA // 2:NA, :]
                low = kqv[:, q, 0:NA // 2, :][:, ::-1, ::-1]
                for c, op in ((0, ALU.add), (1, ALU.subtract)):
                    tt(kfold[:, c, q].rearrange("p (a r) -> p a r", r=NR), high, low, op).then_inc(k_folded, 1)
            dve.wait_ge(kf_done, 1)
            for c in range(2):
                tt(kspec[:, c], bank[4][:].rearrange("p (f h) -> p f h", f=FT), cols(rot[:, c], H), ALU.mult).then_inc(kr_turned, 1)
            dve.wait_ge(kf_done, 2)
            for c, k in ((0, 2), (1, 0)):
                dve.wait_ge(kr_turned, c + 1)
                for ft in range(FT):
                    last = stt(kspec[:, c, ft], bank[7][:, H * ft:H * ft + H], rot[:, k, ft:ft + 1], kspec[:, c, ft],
                               ALU.mult, ALU.add)
                last.then_inc(k_ready, 1)

            def product(i, s):
                if past(i, 2):
                    dve.wait_ge(eo_done, i - 1)
                else:
                    dve.wait_ge(fwd_out, FT)
                    dve.wait_ge(k_ready, 2)
                tt(term[:, s, 0], spectrum(0, i), kspec[:, 0], ALU.mult).then_inc(terms, 1)
                tt(term[:, s, 1], spectrum(1, i), kspec[:, 1], ALU.mult).then_inc(terms, 1)
                dve.wait_ge(terms, 2 * i + 2)
                tt(yspec[:, s, 0], term[:, s, 0], term[:, s, 1], ALU.subtract).then_inc(re_done, 1)

            def unfold(i, s):
                dve.wait_ge(odd_out, i + 1)
                if past(i, 2):
                    dve.wait_ge(gelu_done, i - 1)
                tt(ypre[:, s, M:L], bank[s][:, 0:M], odd[:, s], ALU.add)
                tt(ypre[:, s, 0:M], bank[s][:, 0:M], odd[:, s], ALU.subtract).then_inc(y_done, 1)

            def gated(i, s):
                dve.wait_ge(tanh_done, i + 1)
                if past(i, 2):
                    dve.wait_ge(x1_done, i - 1)
                for k in range(2):
                    a_ = bank[2 + 2 * s + k][:].rearrange("p (t o) -> p t o", t=2)[:, :, 0:H]
                    last = stt(tbuf[:, s, 2 * k:2 * k + 2, :], th[:, s, 2 * k:2 * k + 2, :], 1.0, a_, ALU.add, ALU.mult)
                last.then_inc(t_done, 1)

            def add_u(i, s):
                dve.wait_ge(t_done, i + 1)
                tt(tbuf[:, s], tbuf[:, s], seq(u_tok, i), ALU.add).then_inc(tu_done, 1)

            def moments2(i, s):
                dve.wait_ge(tu_done, i + 1)
                moments(T * i, lambda t: tbuf[:, s, t], st[:, s, 0:T], mv[:, s, 0:T], bn2, mv2_s)

            def add_x(i, s):
                dve.wait_ge(w2_done, i + 1)
                tt(seq(x_tok, i), seq(x_tok, i), tbuf[:, s], ALU.add).then_inc(x1_done, 1)

            def moments3(i, s):
                dve.wait_ge(x1_done, i + 1)
                moments(T * i, lambda t: tile_of(x_tok, i, t), st3[:, s], mv3[:, s], bn3, mv3_s)

            def v_low(i, s):
                dve.wait_ge(vh_done, i + 1)
                tt(vl[:, s], turn_bank(i, s)[:], vh[:, s].bitcast(F32), ALU.subtract).then_inc(vl_done, 1)

            def hidden(i, s, j):
                n = J * i + j
                r = (J * s + j) % 2
                dve.wait_ge(silu_done, n + 1)
                if j == 0 and past(i, 2):
                    dve.wait_ge(dn_done, i - 1)
                tt(hb[:, s, j], sg[:, r], bank[GATE_UP[r][1]][:], ALU.mult).then_inc(h_done, 1)

            def moments4(i, s):
                dve.wait_ge(dn_done, i + 1)
                moments(T * i, lambda t: bank[4 + s][:, H * t:H * t + H], st[:, s, 0:T], mv[:, s, 0:T], bn4, mv4)

            def add_out(i, s):
                dve.wait_ge(w4_done, i + 1)
                tt(seq(x_tok, i), seq(x_tok, i), tbuf[:, s], ALU.add).then_inc(o_done, 1)

            def step(i, s, older=True):
                unfold(i, s)
                product(i + 2, s)
                gated(i - 1, 1 - s)
                add_u(i - 1, 1 - s)
                moments2(i - 1, 1 - s)
                if older:
                    add_x(i - 2, s)

            product(0, 0)
            product(1, 1)
            unfold(0, 0)
            dve.wait_ge(fwd_out, 2 * FT)
            product(2, 0)
            step(1, 1, older=False)
            dve.wait_ge(fwd_out, FT * (B // PAIR))
            unit_steps(dve, 2, B - 2, step)
            moments3(0, 0)
            moments3(1, 1)
            unfold(B - 2, 0)
            gated(B - 3, 1)
            add_u(B - 3, 1)
            moments2(B - 3, 1)
            unfold(B - 1, 1)
            v_low(0, 0)
            add_x(B - 4, 0)
            gated(B - 2, 0)
            add_u(B - 2, 0)
            moments2(B - 2, 0)
            hidden(0, 0, 0)
            add_x(B - 3, 1)
            gated(B - 1, 1)
            add_u(B - 1, 1)
            hidden(0, 0, 1)
            moments3(2, 0)
            moments2(B - 1, 1)
            v_low(1, 1)
            hidden(0, 0, 2)
            add_x(B - 2, 0)

            def ffn_step(i, s, older=True, more=2):
                hidden(i, s, 0)
                if more >= 2:
                    moments3(i + 2, s)
                hidden(i, s, 1)
                if more >= 1:
                    v_low(i + 1, 1 - s)
                if older:
                    add_out(i - 2, s)
                else:
                    add_x(B - 1, 1)
                moments4(i - 1, 1 - s)
                hidden(i, s, 2)
            ffn_step(1, 1, older=False)
            unit_steps(dve, 2, B - 2, ffn_step)
            ffn_step(B - 2, 0, more=1)
            ffn_step(B - 1, 1, more=0)
            add_out(B - 2, 0)
            moments4(B - 1, 1)
            add_out(B - 1, 1)

        @block.tensor
        def _(pe):
            mm = nc.tensor.matmul
            pe.wait_ge(fwd_in, 16)

            def forward(j, ft):
                if ft == 0:
                    pe.wait_ge(fold_ready if j else fold0_ready, max(j, 1))
                if j == 1 or j == 2:
                    pe.wait_ge(fwd_out, FT * (j - 1) + ft + 1)
                if j == 3:
                    pe.wait_ge(*((kq_out, 2), (kt_out, 1), (k_ready, 2), (k_ready, 2))[ft])
                for c in range(2):
                    for mt in range(MT):
                        last = mm(bank[fwd_bank(j, ft)][:, PAIR * H * c:PAIR * H * (c + 1)], fwd[:, c, mt, P * ft:P * ft + P],
                                  fold[:, c, mt, PAIR * j:PAIR * j + PAIR, :].rearrange("p b h -> p (b h)"),
                                  start=(mt == 0), stop=(mt == MT - 1))
                last.then_inc(fwd_done, 1)

            for ft in range(FT):
                forward(0, ft)
            for ft in range(FT):
                forward(1, ft)
            pe.wait_ge(g_b, 1)
            pe.wait_ge(g_pp, 2)
            for h in range(HQ):
                last = mm(bank[4 + h // 16][0:2 * NA, NR * (h % 16):NR * (h % 16) + NR], p_mat[:, h, :], b_mat[:, h, :],
                          start=True, stop=True)
                if h % 16 == 15:
                    last.then_inc(k2_done, 1)
            pe.wait_ge(misc_in, 96)
            pe.wait_ge(k2_out, 4)
            for r in range(NR):
                last = nc.tensor.transpose(bank[4 + r // 16][0:HQ, 2 * NA * (r % 16):2 * NA * (r % 16) + 2 * NA],
                                           k2s[:, :, r], ident[0:2 * NA, 0:2 * NA])
                if r % 16 == 15:
                    last.then_inc(kq_done, 1)
            forward(2, 0)
            forward(2, 1)
            pe.wait_ge(k_folded, 4)
            for c in range(2):
                for mt in range(MT):
                    for q in range(2):
                        n = (c * MT + mt) * 2 + q
                        last = nc.tensor.transpose(bank[6][:, HQ * n:HQ * n + HQ], kfold[:, c, q, P * mt:P * mt + P],
                                                   ident[0:HQ, 0:HQ])
            last.then_inc(kt_done, 1)
            forward(2, 2)
            pe.wait_ge(kt_out, 1)
            for c in range(2):
                for ft in range(FT):
                    for mt in range(MT):
                        last = mm(bank[4 + 3 * c][:, H * ft:H * ft + H], fwd[:, c, mt, P * ft:P * ft + P], kfold_t[:, c, mt, :],
                                  start=(mt == 0), stop=(mt == MT - 1))
                last.then_inc(kf_done, 1)
            forward(2, 3)
            forward(3, 0)
            forward(3, 1)

            def inverse(i, s):
                pe.wait_ge(re_done, i + 1)
                if past(i, 2):
                    pe.wait_ge(y_done, i - 1)
                else:
                    pe.wait_ge(fwd_out, 2 * FT + i + 1)
                for c in range(2):
                    if c == 1:
                        pe.wait_ge(im_done, i + 1)
                    for ft in range(FT):
                        last = mm(bank[s][:, M * c:M * c + M], yspec[:, s, c, ft, :], inv[:, c, ft, :],
                                  start=(ft == 0), stop=(ft == FT - 1))
                last.then_inc(eo_done, 1)

            def linear(i, s):
                pe.wait_ge(gelu_done, i + 1)
                if past(i, 2):
                    pe.wait_ge(t_done, i - 1)
                for t in range(T):
                    o = bank[2 + 2 * s + t // 2][:, 2 * H * (t % 2):2 * H * (t % 2) + 2 * H]
                    mm(o, ones3[:], bias_b[:, 2], start=True, stop=False)
                    last = mm(o, yact[:, s, P * t:P * t + P], w_out[:], start=False, stop=True)
                last.then_inc(z_done, 1)

            def turn_v(i, s):
                pe.wait_ge(v_done, i + 1)
                if past(i, 2):
                    pe.wait_ge(vl_done, i - 1)
                for t in range(T):
                    last = nc.tensor.transpose(turn_bank(i, s)[:, P * t:P * t + P], vbuf[:, s, t, :], ident[:])
                last.then_inc(vt_done, 1)

            def gate_up(i, s, j):
                n = J * i + j
                r = (J * s + j) % 2
                if j == 0:
                    pe.wait_ge(vl_done, i + 1)
                if past(n, 2):
                    pe.wait_ge(h_done, n - 1)
                for k in range(2):
                    o = slice(HID * k + P * j, HID * k + P * j + P)
                    mm(bank[GATE_UP[r][k]][:], wh[:, o], vh[:, s, :], start=True, stop=False)
                    mm(bank[GATE_UP[r][k]][:], wh[:, o], vl[:, s, :], start=False, stop=False)
                    last = mm(bank[GATE_UP[r][k]][:], wl[:, o], vh[:, s, :], start=False, stop=True)
                last.then_inc(gu_done, 1)

            def down(i, s):
                pe.wait_ge(h_done, J * i + J)
                if past(i, 2):
                    pe.wait_ge(w4_done, i - 1)
                for t in range(T):
                    for j in range(J):
                        last = mm(bank[4 + s][:, H * t:H * t + H], hb[:, s, j, P * t:P * t + P],
                                  w_ffn[:, 2 * HID + H * j:2 * HID + H * j + H], start=(j == 0), stop=(j == J - 1))
                last.then_inc(dn_done, 1)

            pe.wait_ge(inv_in, 16)
            inverse(0, 0)
            forward(3, 2)
            forward(3, 3)
            pe.wait_ge(fwd_out, 3 * FT)
            pe.wait_ge(bias_ready, 1)
            pe.wait_ge(w_half, 1)
            pe.wait_ge(setup_p, 4)

            def step(i, s):
                inverse(i + 1, 1 - s)
                linear(i, s)
            step(0, 0)
            pe.wait_ge(fwd_out, 4 * FT)
            step(1, 1)
            unit_steps(pe, 2, B - 2, step)
            pe.wait_ge(ffn_wl, 1)
            step(B - 2, 0)
            turn_v(0, 0)
            linear(B - 1, 1)
            pe.wait_ge(y_done, B)
            gate_up(0, 0, 0)
            turn_v(1, 1)
            pe.wait_ge(t_done, B - 1)
            gate_up(0, 0, 1)
            gate_up(0, 0, 2)

            def ffn_step(i, s, more=True):
                gate_up(i, s, 0)
                gate_up(i, s, 1)
                if more:
                    turn_v(i + 1, 1 - s)
                down(i - 1, 1 - s)
                gate_up(i, s, 2)
            pe.wait_ge(t_done, B)
            ffn_step(1, 1)
            unit_steps(pe, 2, B - 2, ffn_step)
            ffn_step(B - 2, 0)
            ffn_step(B - 1, 1, more=False)
            down(B - 1, 1)


def kernel(L0_attn_x, L0_attn_log_dt, L0_attn_C_re, L0_attn_C_im, L0_attn_log_A_re, L0_attn_A_im, L0_attn_D,
           L0_attn_W, L0_attn_b, L0_ffn_w_gate, L0_ffn_w_up, L0_ffn_w_down):
    import concourse.bacc as bacc
    from concourse.bass_utils import run_bass_kernel_spmd

    def spread(p):
        q = np.asarray(p).reshape(2, HQ, N2).transpose(0, 2, 1)
        return np.stack([q, q], axis=1).reshape(P, HQ)

    x = np.asarray(L0_attn_x)
    log_dt = np.broadcast_to(np.asarray(L0_attn_log_dt)[:, None], (H, N2))
    arrays = {
        "x": np.concatenate([x[:, M - 1::-1], x[:, M:]], axis=1),
        "ssm": np.concatenate([spread(p) for p in (L0_attn_log_A_re, L0_attn_A_im, L0_attn_C_re, L0_attn_C_im, log_dt)], axis=1),
        "d": np.asarray(L0_attn_D).reshape(2, HQ).T,
        "w": np.asarray(L0_attn_W).T,
        "b": np.broadcast_to(np.asarray(L0_attn_b)[None, :], (3, 2 * H)),
        "ffn": np.concatenate([np.asarray(L0_ffn_w_gate).T, np.asarray(L0_ffn_w_up).T,
                               np.asarray(L0_ffn_w_down).T.reshape(J, P, H).transpose(1, 0, 2).reshape(P, HID)], axis=1),
    }
    arrays.update(shape_constants())
    nc = bacc.Bacc("TRN2", target_bir_lowering=False, num_devices=1)
    arrays = {f"in_{k}": np.ascontiguousarray(v) for k, v in arrays.items()}
    d = {k[3:]: nc.dram_tensor(k, v.shape, mybir.dt.from_np(v.dtype), kind="ExternalInput").ap() for k, v in arrays.items()}
    d["out"] = nc.dram_tensor("out", (B, L, H), F32, kind="ExternalOutput").ap()
    build(nc, d)
    got = run_bass_kernel_spmd(nc, [arrays], core_ids=[0]).results[0]["out"]
    return np.concatenate([got[:, M - 1::-1], got[:, M:]], axis=1)
```

```python
from contextlib import ExitStack

import numpy as np

import concourse.bass as bass
from concourse import mybir

B, L, H, N2 = 8, 512, 128, 32
HID = 384
P = 128
M = L // 2
MT = M // P
F = L
FT = F // P
T = L // P
J = HID // P
HQ = H // 2
NR = 32
NA = L // NR
NA1 = NA + 1
PAIR = 2
EPS = 1e-5
SCALE = 1.0 / 127.0
ROUND = 1.5 * 2.0**23
TWO_PI = 6.283185
UNIT = T * H

F32 = mybir.dt.float32
F32R = mybir.dt.float32r
BF16 = mybir.dt.bfloat16
I32 = mybir.dt.int32
ALU = mybir.AluOpType
ACT = mybir.ActivationFunctionType


def shape_constants():
    m, f = np.arange(M), np.arange(F)
    angle = np.pi * np.outer(2 * m + 1, 2 * f + 1) / (4.0 * L)
    trig = np.stack([np.cos(angle), np.sin(angle)])
    fwd = trig.reshape(2, MT, P, F).transpose(2, 0, 1, 3).reshape(P, -1)
    inv = trig.transpose(0, 2, 1).reshape(2, FT, P, M).transpose(2, 0, 1, 3).reshape(P, -1)
    turn = np.pi * (2 * f + 1) * (L - 1) / (4.0 * L)
    c0, s0 = np.cos(turn) / L, np.sin(turn) / L
    rot = np.stack([c0, s0, -s0]).reshape(3, FT, P).transpose(2, 0, 1).reshape(P, -1)
    powers = np.concatenate([NR * np.arange(NA), [1], np.arange(NR)])
    is_re = ((np.arange(P) // N2) % 2 == 0)[:, None]
    signs = [is_re * 2.0, is_re * -2.0, ~is_re * -2.0]
    gen = np.concatenate([np.tile(powers, (P, 1)), np.where(is_re, 0.25, 0.0), *signs, np.full((P, 1), np.pi / 2)], axis=1)
    out = {"fwd": fwd, "inv": inv, "rot": rot, "gen": gen, "ident": np.eye(P), "parts3": np.eye(3)}
    return {k: np.ascontiguousarray(v, dtype=np.float32) for k, v in out.items()}


def build(nc, d):
    es = ExitStack()
    with es:
        def sb(name, shape, dt=F32):
            return es.enter_context(nc.sbuf_tensor(name, shape, dt))

        def sem(name):
            return es.enter_context(nc.semaphore(name))

        x_tok = sb("x_tok", [P, B, T, H])
        u_tok = sb("u_tok", [P, B, T, H])
        fold = sb("fold", [P, 2, MT, B, H])
        spec = sb("spec", [P, 2, FT, B, H])
        kspec = sb("kspec", [P, 2, FT, H])
        fwd = sb("fwd", [P, 2, MT, F])
        inv = sb("inv", [P, 2, FT, M])
        rot = sb("rot", [P, 3, FT])
        gen = sb("gen", [P, NA1 + NR + 5])
        ident = sb("ident", [P, P])
        ssm = sb("ssm", [P, 5, HQ])
        d_col = sb("d_col", [HQ, 2])
        w_out = sb("w_out", [H, 2 * H])
        bias3 = sb("bias3", [3, 2 * H])
        parts3 = sb("parts3", [3, 3])
        bias_b = sb("bias_b", [3, 3, 2 * H], BF16)
        ones3 = sb("ones3", [3, P], BF16)
        w_int = sb("w_int", [P, 3 * HID], I32)
        w_ffn = sb("w_ffn", [P, 3 * HID])
        half_neg = sb("half_neg", [P, PAIR * T])
        eps_t = sb("eps_t", [P, PAIR * T])
        zero_t = sb("zero_t", [P, PAIR * T])
        unread = sb("unread", [P, 1])
        held = sb("held", [P, 1])
        small = sb("small", [P, 18, HQ])
        st = sb("st", [P, 2, PAIR * T, 6])
        mv = sb("mv", [P, 2, PAIR * T, 2])
        rs = sb("rs", [P, 2, PAIR * T])
        nb = sb("nb", [P, 2, PAIR * T])
        st3 = sb("st3", [P, 2, T, 6])
        mv3 = sb("mv3", [P, 2, T, 2])
        rs3 = sb("rs3", [P, 2, T])
        nb3 = sb("nb3", [P, 2, T])
        vh = sb("vh", [P, 2, L], F32R)
        vl = sb("vl", [P, 2, L], F32R)
        wh = sb("wh", [P, 2 * HID], F32R)
        wl = sb("wl", [P, 2 * HID], F32R)

        neg_a_re, dt, rate, turns, ea_re, ea_im = (small[:, k] for k in range(6))
        prod = [small[:, 6 + k] for k in range(6)]
        abs2, abs2_inv, ca_re, ca_im, ck_re, ck_im = (small[:, 12 + k] for k in range(6))

        GA, GB = HQ * NA1, HQ * NR
        pool_a = sb("pool_a", [P, 2 * GA + 2 * GA + GA])
        mag_a = pool_a[:, 0:GA].rearrange("p (h k) -> p h k", h=HQ)
        t_a = pool_a[:, GA:2 * GA]
        k_a = pool_a[:, 3 * GA:5 * GA].rearrange("p (v k) -> p v k", v=2)
        ypre = pool_a[:, 0:2 * L].rearrange("p (s l) -> p s l", s=2)
        yact = pool_a[:, 2 * L:4 * L].rearrange("p (s l) -> p s l", s=2)
        th = pool_a[:, 4 * L:6 * L].rearrange("p (s t h) -> p s t h", s=2, t=T)
        tbuf = pool_a[:, 6 * L:9 * L].rearrange("p (s t h) -> p s t h", s=3, t=T)
        odd = pool_a[:, 9 * L:10 * L].rearrange("p (s m) -> p s m", s=2)
        pool_b = sb("pool_b", [P, 3 * GB])
        mag_b, t_b, k_b = (pool_b[:, GB * k:GB * (k + 1)] for k in range(3))
        yspec = pool_b[:, 0:4 * UNIT].rearrange("p (s c f h) -> p s c f h", s=2, c=2, f=FT)
        term = pool_b[:, 4 * UNIT:8 * UNIT].rearrange("p (s c f h) -> p s c f h", s=2, c=2, f=FT)
        term_p = pool_b[:, 8 * UNIT:10 * UNIT].rearrange("p (c f h) -> p c f h", c=2, f=FT)
        bias_w = pool_b[0:3, 10 * UNIT:12 * UNIT].rearrange("p (k o) -> p k o", k=4)
        pool_c = sb("pool_c", [P, 3 * GB])
        b_mat = pool_c[:, 0:GB].rearrange("p (h r) -> p h r", h=HQ)
        p_mat = pool_c[:, GB:2 * GB].rearrange("p (h k) -> p h k", h=HQ)
        k2s = pool_c[0:2 * NA, 2 * GB:3 * GB].rearrange("p (h r) -> p h r", h=HQ)
        kq = pool_c[0:HQ, 0:2 * L]
        kfold = pool_c[0:HQ, 2 * L:4 * L].rearrange("p (c q m) -> p c q m", c=2, q=2)
        kfold_t = pool_c[:, 4 * L:5 * L].rearrange("p (c t h) -> p c t h", c=2, t=MT)
        vbuf = pool_c[:, 0:2 * UNIT].rearrange("p (s t h) -> p s t h", s=2, t=T)
        sg = pool_c[:, 2 * UNIT:4 * UNIT].rearrange("p (s l) -> p s l", s=2)
        hb = pool_c[:, 4 * UNIT:10 * UNIT].rearrange("p (s j l) -> p s j l", s=2, j=J)

        bank = [es.enter_context(nc.psum_tensor(f"bank{i}", [P, 512], F32)) for i in range(8)]

        ssm_in = sem("ssm_in")
        gen_in = sem("gen_in")
        fwd_in = sem("fwd_in")
        inv_in = sem("inv_in")
        misc_in = sem("misc_in")
        ffn_in = sem("ffn_in")
        setup_p = sem("setup_p")
        bias_step = sem("bias_step")
        bias_ready = sem("bias_ready")
        w_half = sem("w_half")
        ffn_w = sem("ffn_w")
        ffn_wh = sem("ffn_wh")
        ffn_wl = sem("ffn_wl")
        g_exp = sem("g_exp")
        g_rate = sem("g_rate")
        g_arg_a = sem("g_arg_a")
        g_arg_b = sem("g_arg_b")
        g_mag_a = sem("g_mag_a")
        g_mag_b = sem("g_mag_b")
        g_ta = sem("g_ta")
        g_tb = sem("g_tb")
        g_tb_phase = sem("g_tb_phase")
        g_ka = sem("g_ka")
        g_fa = sem("g_fa")
        g_kb = sem("g_kb")
        g_fb = sem("g_fb")
        g_sin_a = sem("g_sin_a")
        g_sin_b = sem("g_sin_b")
        g_uv = sem("g_uv")
        g_sm = sem("g_sm")
        g_recip = sem("g_recip")
        g_ck = sem("g_ck")
        g_b = sem("g_b")
        g_pp = sem("g_pp")
        g_zero = sem("g_zero")
        k2_done = sem("k2_done")
        k2_out = sem("k2_out")
        kq_done = sem("kq_done")
        kq_out = sem("kq_out")
        kd_added = sem("kd_added")
        k_folded = sem("k_folded")
        kt_done = sem("kt_done")
        kt_out = sem("kt_out")
        kf_done = sem("kf_done")
        kr_turned = sem("kr_turned")
        k_ready = sem("k_ready")
        ln1_bn = sem("ln1_bn")
        ln1_mv = sem("ln1_mv")
        ln1_step = sem("ln1_step")
        ln1_rs = sem("ln1_rs")
        u_ready = sem("u_ready")
        u1_ready = sem("u1_ready")
        fold_ready = sem("fold_ready")
        fold_v = sem("fold_v")
        fwd_done = sem("fwd_done")
        fwd_out = sem("fwd_out")
        terms = sem("terms")
        re_done = sem("re_done")
        terms_p = sem("terms_p")
        im_done = sem("im_done")
        eo_done = sem("eo_done")
        odd_out = sem("odd_out")
        y_done = sem("y_done")
        gelu_done = sem("gelu_done")
        z_done = sem("z_done")
        tanh_done = sem("tanh_done")
        t_done = sem("t_done")
        tu_done = sem("tu_done")
        bn2 = sem("bn2")
        mv2_s = sem("mv2_s")
        step2 = sem("step2")
        rs2 = sem("rs2")
        w2_done = sem("w2_done")
        w2_last = sem("w2_last")
        x1_done = sem("x1_done")
        x1_last = sem("x1_last")
        bn3 = sem("bn3")
        mv3_s = sem("mv3_s")
        step3 = sem("step3")
        rs3_s = sem("rs3_s")
        v_done = sem("v_done")
        vt_done = sem("vt_done")
        vh_done = sem("vh_done")
        vl_done = sem("vl_done")
        gu_done = sem("gu_done")
        silu_done = sem("silu_done")
        h_done = sem("h_done")
        dn_done = sem("dn_done")
        bn4 = sem("bn4")
        mv4 = sem("mv4")
        step4 = sem("step4")
        rs4 = sem("rs4")
        w4_done = sem("w4_done")
        o_done = sem("o_done")
        stored = sem("stored")
        x_in = [sem(f"x_in{j}") for j in range(B // PAIR)]

        pow_a, pow_b = gen[:, 0:NA1], gen[:, NA1:NA1 + NR]
        PH = NA1 + NR

        def rows(ap, n):
            return ap.unsqueeze(1).to_broadcast([P, n, ap.shape[1]])

        def cols(ap, n):
            return ap.unsqueeze(2).to_broadcast([P, ap.shape[1], n])

        def seq(ap, b):
            return ap[:, bass.ds(b, 1), :, :].rearrange("p a t h -> p (a t) h")

        def tile_of(ap, b, t):
            return ap[:, bass.ds(b, 1), t, :].rearrange("p a h -> p (a h)")

        def spectrum(c, b):
            return spec[:, c, :, bass.ds(b, 1), :].rearrange("p f a h -> p (f a) h")

        def fold_pair(tt, j, done):
            b = slice(PAIR * j, PAIR * j + PAIR)
            for mt in range(MT):
                for c, op in ((0, ALU.add), (1, ALU.subtract)):
                    last = tt(fold[:, c, mt, b, :], u_tok[:, b, MT + mt, :], u_tok[:, b, mt, :], op)
            last.then_inc(done, 1)

        def past(i, n):
            return not isinstance(i, int) or i >= n

        def among_last(i, n):
            return isinstance(i, int) and i >= B - n

        GATE, UP = (0, 1), (6, 2, 7)

        def turn_bank(i, s):
            return bank[6 + s] if not past(i, 2) else bank[3]

        def out_tile(i, s, t):
            b = bank[(5, 3, 6, 0)[t]] if among_last(i, 1) else bank[4 + s]
            return b[:, H * t:H * t + H]

        def t_slot(i, s):
            return 2 * (B - 1 - i) if among_last(i, 2) else s

        def unit_steps(eng, lo, hi, step):
            with eng.Fori(lo // 2, hi // 2) as k:
                step(2 * k, 0)
                step(2 * k + 1, 1)

        block = es.enter_context(nc.Block())

        @block.sync
        def _(sp):
            sp.dma_start(ssm[:], d["ssm"].rearrange("p (k h) -> p k h", k=5)).then_inc(ssm_in, 16)
            xd = d["x"].rearrange("b (t p) h -> p b t h", p=P)

            def load_x(j):
                for b in range(PAIR * j, PAIR * j + PAIR):
                    sp.dma_start(x_tok[:, b], xd[:, b]).then_inc(x_in[j], 16)
            load_x(0)
            sp.dma_start(gen[:], d["gen"]).then_inc(gen_in, 16)
            load_x(1)
            sp.dma_start(fwd[:], d["fwd"].rearrange("p (c t f) -> p c t f", c=2, t=MT)).then_inc(fwd_in, 16)
            sp.dma_start(bias3[:], d["b"]).then_inc(misc_in, 16)
            sp.dma_start(parts3[:], d["parts3"]).then_inc(misc_in, 16)
            sp.dma_start(ident[:], d["ident"]).then_inc(misc_in, 16)
            sp.dma_start(rot[:], d["rot"].rearrange("p (c t) -> p c t", c=3)).then_inc(misc_in, 16)
            sp.dma_start(d_col[:], d["d"]).then_inc(misc_in, 16)
            sp.dma_start(w_out[:], d["w"]).then_inc(misc_in, 16)
            load_x(2)
            sp.dma_start(w_int[:], d["ffn"]).then_inc(ffn_in, 16)
            load_x(3)
            sp.dma_start(inv[:], d["inv"].rearrange("p (c t m) -> p c t m", c=2, t=FT)).then_inc(inv_in, 16)
            od = d["out"].rearrange("b (t p) h -> p b t h", p=P)
            with sp.Fori(0, B - 1) as i:
                sp.wait_ge(o_done, i + 1)
                sp.dma_start(od[:, bass.ds(i, 1)], x_tok[:, bass.ds(i, 1)]).then_inc(stored, 16)
            for k in range(2):
                sp.wait_ge(o_done, B + k)
                half = slice(T // 2 * k, T // 2 * (k + 1))
                sp.dma_start(od[:, B - 1, half], x_tok[:, B - 1, half]).then_inc(stored, 16)
            sp.wait_ge(stored, 16 * (B + 1))

        @block.gpsimd
        def _(pool):
            tt = nc.gpsimd.tensor_tensor
            nc.gpsimd.memset(half_neg[:], -0.5).then_inc(setup_p, 1)
            nc.gpsimd.memset(eps_t[:], EPS).then_inc(setup_p, 1)
            nc.gpsimd.memset(zero_t[:], 0.0).then_inc(setup_p, 1)
            nc.gpsimd.memset(ones3[:], 1.0).then_inc(setup_p, 1)
            nc.gpsimd.memset(p_mat, 0.0).then_inc(g_zero, 1)
            pool.wait_ge(setup_p, 4)

            def rstd(n, mean_var, rs_, nb_, step, done):
                k = rs_.shape[1]
                tt(rs_, mean_var[:, :, 1], eps_t[:, 0:k], ALU.add).then_inc(step, 1)
                pool.wait_ge(step, 3 * n + 1)
                tt(rs_, rs_, half_neg[:, 0:k], ALU.pow).then_inc(step, 1)
                pool.wait_ge(step, 3 * n + 2)
                tt(nb_, mean_var[:, :, 0], rs_, ALU.mult).then_inc(step, 1)
                pool.wait_ge(step, 3 * n + 3)
                tt(nb_, zero_t[:, 0:k], nb_, ALU.subtract).then_inc(done, 1)

            def ln1_rstd(j):
                pool.wait_ge(ln1_mv, j + 1)
                if j >= 2:
                    pool.wait_ge(u_ready, j - 1)
                rstd(j, mv[:, j % 2], rs[:, j % 2], nb[:, j % 2], ln1_step, ln1_rs)

            def ln1_fold(j):
                pool.wait_ge(u_ready, j + 1)
                fold_pair(nc.gpsimd.tensor_tensor, j, fold_ready)

            a_im, cr, ci = ssm[:, 1], ssm[:, 2], ssm[:, 3]
            count = [0]

            def s_op(out, a, b, op):
                count[0] += 1
                tt(out, a, b, op).then_inc(g_sm, 1)

            def s_wait():
                pool.wait_ge(g_sm, count[0])

            pool.wait_ge(g_exp, 2)
            pool.wait_ge(ssm_in, 16)
            s_op(prod[0], neg_a_re, neg_a_re, ALU.mult)
            s_op(prod[1], a_im, a_im, ALU.mult)
            s_wait()
            s_op(abs2, prod[0], prod[1], ALU.add)
            s_op(prod[2], cr, neg_a_re, ALU.mult)
            s_op(prod[3], ci, a_im, ALU.mult)
            s_op(prod[4], cr, a_im, ALU.mult)
            s_op(prod[5], ci, neg_a_re, ALU.mult)
            s_wait()
            s_op(ca_re, prod[3], prod[2], ALU.subtract)
            s_op(ca_im, prod[4], prod[5], ALU.add)
            s_wait()
            ln1_rstd(0)
            pool.wait_ge(g_recip, 1)
            s_op(ca_re, ca_re, abs2_inv, ALU.mult)
            s_op(ca_im, ca_im, abs2_inv, ALU.mult)
            ln1_rstd(1)
            pool.wait_ge(gen_in, 16)
            pool.wait_ge(g_rate, 2)
            tt(mag_b.rearrange("p (h r) -> p h r", h=HQ), cols(rate, NR), rows(pow_b, HQ), ALU.mult).then_inc(g_arg_b, 1)
            ln1_fold(1)
            ln1_rstd(2)
            pool.wait_ge(g_kb, 1)
            pool.wait_ge(g_tb_phase, 1)
            tt(k_b, t_b, k_b, ALU.subtract).then_inc(g_fb, 1)
            pool.wait_ge(g_mag_a, 1)
            pool.wait_ge(g_sin_a, 2)
            er = mag_a[:, :, NA]
            sin_a = k_a.rearrange("p v (h k) -> p v h k", h=HQ)
            s_op(ea_re, er, sin_a[:, 1, :, NA], ALU.mult)
            s_op(ea_im, er, sin_a[:, 0, :, NA], ALU.mult)
            s_wait()
            nc.gpsimd.tensor_scalar(ea_re, ea_re, -1.0, None, ALU.add).then_inc(g_sm, 1)
            count[0] += 1
            s_wait()
            s_op(prod[0], ca_re, ea_re, ALU.mult)
            s_op(prod[1], ca_im, ea_im, ALU.mult)
            s_op(prod[2], ca_re, ea_im, ALU.mult)
            s_op(prod[3], ca_im, ea_re, ALU.mult)
            s_wait()
            tt(ck_re, prod[0], prod[1], ALU.add).then_inc(g_ck, 1)
            tt(ck_im, prod[2], prod[3], ALU.subtract).then_inc(g_ck, 1)
            pool.wait_ge(g_mag_b, 1)
            pool.wait_ge(g_sin_b, 1)
            tt(b_mat, mag_b.rearrange("p (h r) -> p h r", h=HQ), k_b.rearrange("p (h r) -> p h r", h=HQ),
               ALU.mult).then_inc(g_b, 1)
            ln1_rstd(3)
            pool.wait_ge(ffn_w, 1)
            pool.wait_ge(ffn_wh, 1)
            tt(wl[:], w_ffn[:, 0:2 * HID], wh[:].bitcast(F32), ALU.subtract).then_inc(ffn_wl, 1)
            ln1_fold(3)

            def product(i, s):
                pool.wait_ge(k_ready, 1)
                if past(i, 2):
                    pool.wait_ge(eo_done, i - 1)
                else:
                    pool.wait_ge(fwd_out, FT)
                if past(i, 1):
                    pool.wait_ge(im_done, i)
                tt(term_p[:, 1], spectrum(1, i), kspec[:, 0], ALU.mult).then_inc(terms_p, 1)
                if not past(i, 1):
                    pool.wait_ge(k_ready, 2)
                tt(term_p[:, 0], spectrum(0, i), kspec[:, 1], ALU.mult).then_inc(terms_p, 1)
                pool.wait_ge(terms_p, 2 * i + 2)
                tt(yspec[:, s, 1], term_p[:, 0], term_p[:, 1], ALU.add).then_inc(im_done, 1)

            def rstd2(i, s):
                pool.wait_ge(mv2_s, i + 1)
                if among_last(i, 2):
                    pool.wait_ge(w2_done, i - 1)
                rstd(i, mv[:, s, 0:T], rs[:, s, 0:T], nb[:, s, 0:T], step2, rs2)

            def rstd3(i, s):
                pool.wait_ge(mv3_s, i + 1)
                rstd(i, mv3[:, s], rs3[:, s], nb3[:, s], step3, rs3_s)

            def rstd4(i, s):
                pool.wait_ge(mv4, i + 1)
                rstd(i, mv[:, s, 0:T], rs[:, s, 0:T], nb[:, s, 0:T], step4, rs4)

            def rstd4_last(half):
                pool.wait_ge(mv4, B + half)
                k = slice(T // 2 * half, T // 2 * (half + 1))
                tt(rs[:, 1, k], mv[:, 1, k, 1], eps_t[:, k], ALU.add).then_inc(step4, 1)
                pool.wait_ge(step4, 3 * (B - 1) + half + 1)
                tt(rs[:, 1, k], rs[:, 1, k], half_neg[:, k], ALU.pow).then_inc(rs4, 1)

            product(0, 0)
            product(1, 1)
            pool.wait_ge(fwd_out, 2 * FT)
            product(2, 0)

            def step(i, s):
                rstd2(i - 2, s)
                product(i + 2, s)
            product(3, 1)
            pool.wait_ge(fwd_out, FT * (B // PAIR))
            pool.wait_ge(u_ready, B // PAIR)
            unit_steps(pool, 2, B - 2, step)
            rstd3(0, 0)
            rstd3(1, 1)
            rstd2(B - 4, 0)
            rstd2(B - 3, 1)
            rstd3(2, 0)
            rstd2(B - 2, 0)
            rstd3(3, 1)
            rstd2(B - 1, 1)

            def norm2_add_x(i, s):
                pool.wait_ge(rs2, i + 1)
                pool.wait_ge(w2_done, i)
                k = t_slot(i, s)
                for t in range(T):
                    last = nc.gpsimd.tensor_scalar(tbuf[:, k, t], tbuf[:, k, t], rs[:, s, t:t + 1], nb[:, s, t:t + 1],
                                                   ALU.mult, ALU.add)
                last.then_inc(w2_done, 1)
                pool.wait_ge(w2_done, i + 1)
                tt(seq(x_tok, i), seq(x_tok, i), tbuf[:, k], ALU.add).then_inc(x1_done, 2)

            def ffn_step(i, s):
                rstd3(i + 2, s)
                rstd4(i - 1, 1 - s)
            norm2_add_x(B - 2, 0)
            rstd4(0, 0)
            unit_steps(pool, 2, B - 2, ffn_step)
            rstd4(B - 3, 1)
            rstd4(B - 2, 0)
            rstd4_last(0)
            rstd4_last(1)

        @block.scalar
        def _(act):
            a = nc.scalar.activation
            act.wait_ge(ssm_in, 16)
            a(neg_a_re, ssm[:, 0], ACT.Exp).then_inc(g_exp, 1)
            a(dt, ssm[:, 4], ACT.Exp).then_inc(g_exp, 1)
            act.wait_ge(g_arg_a, 1)
            a(mag_a, mag_a, ACT.Exp).then_inc(g_mag_a, 1)
            def normalise(src, dst, rs_, nb_, done):
                n = rs_.shape[1]
                for t in range(n):
                    last = a(dst(t), src(t), ACT.Identity, scale=rs_[:, t:t + 1], bias=nb_[:, t:t + 1])
                last.then_inc(done, 1)

            def load_tables(f):
                a(unread[:, 0:1], eps_t[:, 0:1], f)

            def ln1_norm(j):
                act.wait_ge(ln1_rs, j + 1)
                n = T if j in (0, 2) else PAIR * T
                normalise(lambda n: tile_of(x_tok, PAIR * j + n // T, n % T), lambda n: tile_of(u_tok, PAIR * j + n // T, n % T),
                          rs[:, j % 2, 0:n], nb[:, j % 2, 0:n], u_ready)

            def evacuate(j, lo=0, hi=FT):
                for ft in range(lo, hi):
                    act.wait_ge(fwd_done, FT * j + ft + 1)
                    a(spec[:, :, ft, PAIR * j:PAIR * j + PAIR, :], bank[ft][:].rearrange("p (c b h) -> p c b h", c=2, b=PAIR),
                      ACT.Copy).then_inc(fwd_out, 1)

            ln1_norm(0)
            ln1_norm(1)
            act.wait_ge(gen_in, 16)
            act.wait_ge(g_tb, 1)
            a(t_b, t_b, ACT.Identity, bias=gen[:, PH:PH + 1]).then_inc(g_tb_phase, 1)
            act.wait_ge(g_arg_b, 1)
            a(mag_b, mag_b, ACT.Exp).then_inc(g_mag_b, 1)
            evacuate(0, 0, 3)
            load_tables(ACT.Sin)
            act.wait_ge(g_fa, 2)
            a(k_a[:, 0], k_a[:, 0], ACT.Sin, scale=TWO_PI).then_inc(g_sin_a, 1)
            a(k_a[:, 1], k_a[:, 1], ACT.Sin, scale=-TWO_PI, bias=gen[:, PH + 4:PH + 5]).then_inc(g_sin_a, 1)
            evacuate(0, 3)
            ln1_norm(2)
            evacuate(1, 0, 1)
            act.wait_ge(g_fb, 1)
            a(k_b, k_b, ACT.Sin, scale=TWO_PI).then_inc(g_sin_b, 1)
            act.wait_ge(misc_in, 96)
            a(w_out[:, 0:H], w_out[:, 0:H], ACT.Copy, scale=0.5).then_inc(w_half, 1)
            act.wait_ge(ffn_in, 16)
            evacuate(1, 1)
            a(w_ffn[:], w_int[:], ACT.Copy, scale=SCALE).then_inc(ffn_w, 1)
            act.wait_ge(ffn_w, 1)
            a(wh[:], w_ffn[:, 0:2 * HID], ACT.Copy).then_inc(ffn_wh, 1)
            evacuate(2, 0, 3)
            for n in (0, 1, 3):
                act.wait_ge(k2_done, n + 1)
                a(k2s[:, 16 * n:16 * n + 16, :], bank[4 + n][0:2 * NA, :].rearrange("p (h r) -> p h r", h=16),
                  ACT.Copy).then_inc(k2_out, 1)
            ln1_norm(3)
            for c in range(2):
                act.wait_ge(kt_done, c + 1)
                a(kfold_t[:, c].rearrange("p t h -> p (t h)"), bank[6 - c][:, 0:MT * H], ACT.Copy).then_inc(kt_out, 1)
            load_tables(ACT.Gelu)
            evacuate(2, 3)
            evacuate(3, 0, 2)

            def odd_copy(i, s):
                act.wait_ge(eo_done, i + 1)
                if past(i, 2):
                    act.wait_ge(y_done, i - 1)
                a(odd[:, s], bank[s][:, M:2 * M], ACT.Copy).then_inc(odd_out, 1)

            def gelu(i, s):
                act.wait_ge(y_done, i + 1)
                if past(i, 2):
                    act.wait_ge(z_done, i - 1)
                a(yact[:, s], ypre[:, s], ACT.Gelu).then_inc(gelu_done, 1)

            def tanh(i, s):
                act.wait_ge(z_done, i + 1)
                if past(i, 2):
                    act.wait_ge(t_done, i - 1)
                for k in range(2):
                    g = bank[2 + 2 * s + k][:].rearrange("p (t o) -> p t o", t=2)[:, :, H:2 * H]
                    last = a(th[:, s, 2 * k:2 * k + 2, :], g, ACT.Tanh, scale=0.5)
                last.then_inc(tanh_done, 1)

            def norm2(i, s, done=w2_done):
                act.wait_ge(rs2, i + 1)
                k = t_slot(i, s)
                normalise(lambda t: tbuf[:, k, t], lambda t: tbuf[:, k, t], rs[:, s, 0:T], nb[:, s, 0:T], done)

            def norm3(i, s):
                act.wait_ge(rs3_s, i + 1)
                if past(i, 2):
                    act.wait_ge(vt_done, i - 1)
                normalise(lambda t: tile_of(x_tok, i, t), lambda t: vbuf[:, s, t], rs3[:, s], nb3[:, s], v_done)

            def norm4(i, s):
                act.wait_ge(rs4, i + 1)
                normalise(lambda t: out_tile(i, s, t), lambda t: tbuf[:, 1 - s, t], rs[:, s, 0:T], nb[:, s, 0:T], w4_done)

            def v_high(i, s):
                act.wait_ge(vt_done, i + 1)
                if past(i, 2):
                    act.wait_ge(gu_done, J * i - J)
                a(vh[:, s], turn_bank(i, s)[:], ACT.Copy).then_inc(vh_done, 1)

            def silu(i, s, j):
                n = J * i + j
                r = (J * s + j) % 2
                act.wait_ge(gu_done, n + 1)
                if past(n, 2):
                    act.wait_ge(h_done, n - 1)
                a(sg[:, r], bank[GATE[r]][:], ACT.Silu).then_inc(silu_done, 1)

            def step(i, s, older=True):
                odd_copy(i, s)
                gelu(i, s)
                tanh(i - 1, 1 - s)
                if older:
                    norm2(i - 2, s)

            odd_copy(0, 0)
            gelu(0, 0)
            evacuate(3, 2)
            step(1, 1, older=False)
            unit_steps(act, 2, B - 2, step)
            odd_copy(B - 2, 0)
            gelu(B - 2, 0)
            tanh(B - 3, 1)
            odd_copy(B - 1, 1)
            norm3(0, 0)
            gelu(B - 1, 1)
            tanh(B - 2, 0)
            v_high(0, 0)
            load_tables(ACT.Silu)
            norm3(1, 1)
            silu(0, 0, 0)
            v_high(1, 1)
            norm2(B - 4, 0)
            silu(0, 0, 1)
            tanh(B - 1, 1)
            silu(0, 0, 2)
            norm3(2, 0)

            def ffn_step(i, s, more=2):
                silu(i, s, 0)
                silu(i, s, 1)
                if more >= 1:
                    v_high(i + 1, 1 - s)
                norm4(i - 2, s)
                silu(i, s, 2)
                if more >= 2:
                    norm3(i + 2, s)
            silu(1, 1, 0)
            norm2(B - 3, 1)
            silu(1, 1, 1)
            v_high(2, 0)
            norm3(3, 1)
            silu(1, 1, 2)
            norm2(B - 1, 1, done=w2_last)
            unit_steps(act, 2, B - 2, ffn_step)
            ffn_step(B - 2, 0, more=1)
            ffn_step(B - 1, 1, more=0)
            norm4(B - 2, 0)

        @block.vector
        def _(dve):
            tt, ts, stt = nc.vector.tensor_tensor, nc.vector.tensor_scalar, nc.vector.scalar_tensor_tensor

            def moments(n, src, st_, mv_, bn, done):
                k = st_.shape[1]
                for t in range(k):
                    nc.vector.bn_stats(st_[:, t, :], src(t)).then_inc(bn, 1)
                dve.wait_ge(bn, n + k)
                nc.vector.memset(held[:], 0.0)
                for t in range(k):
                    last = nc.vector.bn_aggr(mv_[:, t, :], st_[:, t, :])
                last.then_inc(done, 1)

            def ln1_moments(j):
                dve.wait_ge(x_in[j], 16 * PAIR)
                if j >= 2:
                    dve.wait_ge(ln1_rs, j - 1)
                moments(PAIR * T * j, lambda n: tile_of(x_tok, PAIR * j + n // T, n % T), st[:, j % 2], mv[:, j % 2],
                        ln1_bn, ln1_mv)

            dve.wait_ge(g_exp, 2)
            stt(rate, neg_a_re, -1.0, dt, ALU.mult, ALU.mult).then_inc(g_rate, 1)
            stt(turns, ssm[:, 1], float(1 / (2 * np.pi)), dt, ALU.mult, ALU.mult).then_inc(g_rate, 1)
            ln1_moments(0)
            dve.wait_ge(g_rate, 2)
            dve.wait_ge(gen_in, 16)
            dve.wait_ge(g_sm, 3)
            nc.vector.reciprocal(abs2_inv, abs2).then_inc(g_recip, 1)
            tt(mag_a, cols(rate, NA1), rows(pow_a, HQ), ALU.mult).then_inc(g_arg_a, 1)
            ln1_moments(1)

            def ln1_second(j):
                dve.wait_ge(ln1_rs, j + 1)
                b = PAIR * j + 1
                for t in range(T):
                    last = ts(u_tok[:, b, t], x_tok[:, b, t], rs[:, 0, T + t:T + t + 1], nb[:, 0, T + t:T + t + 1],
                              ALU.mult, ALU.add)
                last.then_inc(u1_ready, 1)

            def ln1_fold(j):
                dve.wait_ge(u1_ready, j // 2 + 1)
                dve.wait_ge(u_ready, j + 1)
                fold_pair(tt, j, fold_v)
            ln1_second(0)
            ln1_fold(0)
            tt(t_b.rearrange("p (h r) -> p h r", h=HQ), cols(turns, NR), rows(pow_b, HQ), ALU.mult).then_inc(g_tb, 1)
            ln1_moments(2)
            tt(t_a.rearrange("p (h k) -> p h k", h=HQ), cols(turns, NA1), rows(pow_a, HQ), ALU.mult).then_inc(g_ta, 1)
            dve.wait_ge(g_tb_phase, 1)
            ts(k_b, t_b, ROUND, -ROUND, ALU.add, ALU.add).then_inc(g_kb, 1)
            dve.wait_ge(g_ta, 1)
            ts(k_a[:, 1], t_a, ROUND, -ROUND, ALU.add, ALU.add).then_inc(g_ka, 1)
            dve.wait_ge(g_ka, 1)
            tt(k_a[:, 0], t_a, k_a[:, 1], ALU.subtract).then_inc(g_fa, 1)
            dve.wait_ge(g_fa, 1)
            stt(k_a[:, 1], k_a[:, 0], -1.0, k_a[:, 0], ALU.mult, ALU.max).then_inc(g_fa, 1)
            ln1_second(2)
            dve.wait_ge(g_mag_a, 1)
            sin_a = k_a.rearrange("p v (h k) -> p v h k", h=HQ)
            for v in range(2):
                dve.wait_ge(g_sin_a, v + 1)
                tt(sin_a[:, v, :, 0:NA], mag_a[:, :, 0:NA], sin_a[:, v, :, 0:NA], ALU.mult).then_inc(g_uv, 1)
            ln1_fold(2)
            dve.wait_ge(g_ck, 2)
            ts(prod[2], ck_re, gen[:, PH + 1:PH + 2], None, ALU.mult).then_inc(g_uv, 1)
            ts(prod[3], ck_re, gen[:, PH + 3:PH + 4], None, ALU.mult).then_inc(g_uv, 1)
            dve.wait_ge(g_uv, 4)
            stt(prod[4], ck_im, gen[:, PH + 3:PH + 4], prod[2], ALU.mult, ALU.add).then_inc(g_uv, 1)
            stt(prod[5], ck_im, gen[:, PH + 2:PH + 3], prod[3], ALU.mult, ALU.add).then_inc(g_uv, 1)
            dve.wait_ge(g_uv, 6)
            for v, factor in ((1, prod[4]), (0, prod[5])):
                tt(sin_a[:, v, :, 0:NA], sin_a[:, v, :, 0:NA], cols(factor, NA), ALU.mult).then_inc(g_uv, 1)
            dve.wait_ge(g_uv, 8)
            dve.wait_ge(g_zero, 1)
            for q in range(2):
                pp = slice(64 * q, 64 * q + 64)
                tt(p_mat[pp, :, NA * q:NA * q + NA], sin_a[pp, 0, :, 0:NA], sin_a[pp, 1, :, 0:NA], ALU.add).then_inc(g_pp, 1)
            ln1_moments(3)

            dve.wait_ge(misc_in, 96)
            bcount = [0]

            def b_op(ins):
                bcount[0] += 1
                ins.then_inc(bias_step, 1)
                dve.wait_ge(bias_step, bcount[0])
            dve.wait_ge(g_b, 1)
            b_op(ts(bias3[:, 0:H], bias3[:, 0:H], 0.5, None, ALU.mult))
            b_op(nc.vector.tensor_copy(bias_b[:, 0], bias3[:]))
            b_op(tt(bias_w[:, 0], bias3[:], bias_b[:, 0], ALU.subtract))
            b_op(nc.vector.tensor_copy(bias_b[:, 1], bias_w[:, 0]))
            dve.wait_ge(k2_done, 3)
            nc.vector.tensor_copy(k2s[:, 32:48, :], bank[6][0:2 * NA, :].rearrange("p (h r) -> p h r", h=16)).then_inc(k2_out, 1)

            for n in range(2):
                dve.wait_ge(kq_done, n + 1)
                nc.vector.tensor_copy(kq[:, L * n:L * n + L], bank[4 + n][0:HQ, :]).then_inc(kq_out, 1)
            dve.wait_ge(kq_out, 2)
            kqv = kq.rearrange("p (r q a) -> p q a r", r=NR, q=2)
            tt(kq[:, 0:2 * NA:NA], kq[:, 0:2 * NA:NA], d_col[:], ALU.add).then_inc(kd_added, 1)
            dve.wait_ge(kd_added, 1)
            for c, op in ((0, ALU.add), (1, ALU.subtract)):
                for q in range(2):
                    high = kqv[:, q, NA // 2:NA, :]
                    low = kqv[:, q, 0:NA // 2, :][:, ::-1, ::-1]
                    tt(kfold[:, c, q].rearrange("p (a r) -> p a r", r=NR), high, low, op).then_inc(k_folded, 1)
            b_op(tt(bias_w[:, 1], bias_w[:, 0], bias_b[:, 1], ALU.subtract))
            b_op(ts(bias_w[:, 2], bias3[:], parts3[:, 0:1], None, ALU.mult))
            b_op(stt(bias_w[:, 3], bias_w[:, 0], parts3[:, 1:2], bias_w[:, 2], ALU.mult, ALU.add))
            b_op(stt(bias_w[:, 2], bias_w[:, 1], parts3[:, 2:3], bias_w[:, 3], ALU.mult, ALU.add))
            nc.vector.tensor_copy(bias_b[:, 2], bias_w[:, 2]).then_inc(bias_ready, 1)
            dve.wait_ge(kf_done, 1)
            for c in range(2):
                tt(kspec[:, c], bank[4][:].rearrange("p (f h) -> p f h", f=FT), cols(rot[:, c], H),
                   ALU.mult).then_inc(kr_turned, 1)
            dve.wait_ge(kf_done, 2)
            for c, k in ((0, 2), (1, 0)):
                dve.wait_ge(kr_turned, c + 1)
                for ft in range(FT):
                    last = stt(kspec[:, c, ft], bank[7][:, H * ft:H * ft + H], rot[:, k, ft:ft + 1], kspec[:, c, ft],
                               ALU.mult, ALU.add)
                last.then_inc(k_ready, 1)

            def product(i, s):
                if past(i, 2):
                    dve.wait_ge(eo_done, i - 1)
                else:
                    dve.wait_ge(fwd_out, FT)
                    dve.wait_ge(k_ready, 2)
                tt(term[:, s, 0], spectrum(0, i), kspec[:, 0], ALU.mult).then_inc(terms, 1)
                tt(term[:, s, 1], spectrum(1, i), kspec[:, 1], ALU.mult).then_inc(terms, 1)
                dve.wait_ge(terms, 2 * i + 2)
                tt(yspec[:, s, 0], term[:, s, 0], term[:, s, 1], ALU.subtract).then_inc(re_done, 1)

            def unfold(i, s):
                dve.wait_ge(odd_out, i + 1)
                if past(i, 2):
                    dve.wait_ge(gelu_done, i - 1)
                tt(ypre[:, s, M:L], bank[s][:, 0:M], odd[:, s], ALU.add)
                tt(ypre[:, s, 0:M], bank[s][:, 0:M], odd[:, s], ALU.subtract).then_inc(y_done, 1)

            def gated(i, s):
                dve.wait_ge(tanh_done, i + 1)
                if among_last(i, 1):
                    dve.wait_ge(x1_done, B - 3)
                elif past(i, 2) and not among_last(i, 2):
                    dve.wait_ge(x1_done, i - 1)
                for k in range(2):
                    a_ = bank[2 + 2 * s + k][:].rearrange("p (t o) -> p t o", t=2)[:, :, 0:H]
                    last = stt(tbuf[:, t_slot(i, s), 2 * k:2 * k + 2, :], th[:, s, 2 * k:2 * k + 2, :], 1.0, a_,
                               ALU.add, ALU.mult)
                last.then_inc(t_done, 1)

            def add_u(i, s):
                dve.wait_ge(t_done, i + 1)
                tt(tbuf[:, t_slot(i, s)], tbuf[:, t_slot(i, s)], seq(u_tok, i), ALU.add).then_inc(tu_done, 1)

            def moments2(i, s):
                dve.wait_ge(tu_done, i + 1)
                if among_last(i, 2):
                    dve.wait_ge(rs2, i - 1)
                moments(T * i, lambda t: tbuf[:, t_slot(i, s), t], st[:, s, 0:T], mv[:, s, 0:T], bn2, mv2_s)

            def add_x(i, s):
                last = among_last(i, 1)
                if last:
                    dve.wait_ge(w2_last, 1)
                else:
                    dve.wait_ge(w2_done, i + 1)
                tt(seq(x_tok, i), seq(x_tok, i), tbuf[:, t_slot(i, s)], ALU.add).then_inc(x1_last if last else x1_done, 1)

            def moments3(i, s):
                dve.wait_ge(x1_done, i + 1)
                moments(T * i, lambda t: tile_of(x_tok, i, t), st3[:, s], mv3[:, s], bn3, mv3_s)

            def v_low(i, s):
                dve.wait_ge(vh_done, i + 1)
                tt(vl[:, s], turn_bank(i, s)[:], vh[:, s].bitcast(F32), ALU.subtract).then_inc(vl_done, 1)

            def hidden(i, s, j):
                n = J * i + j
                r = (J * s + j) % 2
                dve.wait_ge(silu_done, n + 1)
                if j == 0 and past(i, 2):
                    dve.wait_ge(dn_done, i - 1)
                tt(hb[:, s, j], sg[:, r], bank[UP[j]][:], ALU.mult).then_inc(h_done, 1)

            def moments4(i, s, tiles=range(T), late=0):
                dve.wait_ge(dn_done, i + 1 + late)
                k = slice(tiles[0], tiles[-1] + 1)
                moments(T * i + tiles[0], lambda t: out_tile(i, s, tiles[t]), st[:, s, k], mv[:, s, k], bn4, mv4)

            def add_out(i, s, tiles=slice(0, T), late=0):
                dve.wait_ge(w4_done, i + 1 + late)
                tt(seq(x_tok, i)[:, tiles], seq(x_tok, i)[:, tiles], tbuf[:, 1 - s, tiles], ALU.add).then_inc(o_done, 1)

            def norm4_last(half):
                dve.wait_ge(rs4, B + half)
                for t in range(T // 2 * half, T // 2 * (half + 1)):
                    last = ts(tbuf[:, 0, t], out_tile(B - 1, 1, t), mv[:, 1, t, 0:1], rs[:, 1, t:t + 1], ALU.subtract, ALU.mult)
                last.then_inc(w4_done, 1)

            def step(i, s, older=True):
                unfold(i, s)
                product(i + 2, s)
                gated(i - 1, 1 - s)
                add_u(i - 1, 1 - s)
                moments2(i - 1, 1 - s)
                if older:
                    add_x(i - 2, s)

            product(0, 0)
            product(1, 1)
            unfold(0, 0)
            dve.wait_ge(fwd_out, 2 * FT)
            product(2, 0)
            step(1, 1, older=False)
            dve.wait_ge(fwd_out, FT * (B // PAIR))
            unit_steps(dve, 2, B - 2, step)
            moments3(0, 0)
            unfold(B - 2, 0)
            moments3(1, 1)
            gated(B - 3, 1)
            unfold(B - 1, 1)
            add_u(B - 3, 1)
            moments2(B - 3, 1)
            gated(B - 2, 0)
            v_low(0, 0)
            add_u(B - 2, 0)
            moments3(2, 0)
            moments2(B - 2, 0)
            hidden(0, 0, 0)
            v_low(1, 1)
            add_x(B - 4, 0)
            hidden(0, 0, 1)
            gated(B - 1, 1)
            add_u(B - 1, 1)
            hidden(0, 0, 2)
            moments3(3, 1)
            moments2(B - 1, 1)

            def ffn_step(i, s, more=2):
                hidden(i, s, 0)
                if more >= 2:
                    moments3(i + 2, s)
                hidden(i, s, 1)
                if more >= 1:
                    v_low(i + 1, 1 - s)
                add_out(i - 2, s)
                moments4(i - 1, 1 - s)
                hidden(i, s, 2)
            hidden(1, 1, 0)
            add_x(B - 3, 1)
            hidden(1, 1, 1)
            v_low(2, 0)
            dve.wait_ge(rs2, B - 1)
            moments4(0, 0)
            hidden(1, 1, 2)
            add_x(B - 1, 1)
            dve.wait_ge(x1_last, 1)
            unit_steps(dve, 2, B - 2, ffn_step)
            ffn_step(B - 2, 0, more=1)
            ffn_step(B - 1, 1, more=0)
            moments4(B - 1, 1, (0, 1))
            moments4(B - 1, 1, (2, 3), late=1)
            add_out(B - 2, 0)
            for half in range(2):
                norm4_last(half)
                add_out(B - 1, 1, slice(T // 2 * half, T // 2 * (half + 1)), late=half)

        @block.tensor
        def _(pe):
            mm = nc.tensor.matmul
            pe.wait_ge(fwd_in, 16)
            pe.wait_ge(ln1_rs, 1)
            for n in range(2):
                mm(bank[4][:], fwd[:, 0, 0, 0:P], fwd[:, 0, 0, :], start=True, stop=True)

            def forward(j, ft):
                if ft == 0:
                    pe.wait_ge(fold_v if j % 2 == 0 else fold_ready, j // 2 + 1)
                if j:
                    pe.wait_ge(fwd_out, FT * (j - 1) + ft + 1)
                for c in range(2):
                    for mt in range(MT):
                        last = mm(bank[ft][:, PAIR * H * c:PAIR * H * (c + 1)], fwd[:, c, mt, P * ft:P * ft + P],
                                  fold[:, c, mt, PAIR * j:PAIR * j + PAIR, :].rearrange("p b h -> p (b h)"),
                                  start=(mt == 0), stop=(mt == MT - 1))
                last.then_inc(fwd_done, 1)

            for ft in range(FT):
                forward(0, ft)
            for ft in range(FT):
                forward(1, ft)
            forward(2, 0)
            forward(2, 1)
            forward(2, 2)
            pe.wait_ge(g_b, 1)
            pe.wait_ge(g_pp, 2)
            for h in range(HQ):
                last = mm(bank[4 + h // 16][0:2 * NA, NR * (h % 16):NR * (h % 16) + NR], p_mat[:, h, :], b_mat[:, h, :],
                          start=True, stop=True)
                if h % 16 == 15:
                    last.then_inc(k2_done, 1)
            pe.wait_ge(misc_in, 96)
            pe.wait_ge(k2_out, 4)
            for r in range(NR):
                last = nc.tensor.transpose(bank[4 + r // 16][0:HQ, 2 * NA * (r % 16):2 * NA * (r % 16) + 2 * NA],
                                           k2s[:, :, r], ident[0:2 * NA, 0:2 * NA])
                if r % 16 == 15:
                    last.then_inc(kq_done, 1)
            forward(2, 3)
            for c in range(2):
                pe.wait_ge(k_folded, 2 * c + 2)
                for mt in range(MT):
                    for q in range(2):
                        n = 2 * mt + q
                        last = nc.tensor.transpose(bank[6 - c][:, HQ * n:HQ * n + HQ], kfold[:, c, q, P * mt:P * mt + P],
                                                   ident[0:HQ, 0:HQ])
                last.then_inc(kt_done, 1)
            for c in range(2):
                pe.wait_ge(kt_out, c + 1)
                for ft in range(FT):
                    for mt in range(MT):
                        last = mm(bank[4 + 3 * c][:, H * ft:H * ft + H], fwd[:, c, mt, P * ft:P * ft + P], kfold_t[:, c, mt, :],
                                  start=(mt == 0), stop=(mt == MT - 1))
                last.then_inc(kf_done, 1)
            forward(3, 0)
            forward(3, 1)
            forward(3, 2)

            def inverse(i, s):
                pe.wait_ge(re_done, i + 1)
                if past(i, 2):
                    pe.wait_ge(y_done, i - 1)
                else:
                    pe.wait_ge(fwd_out, 3 * FT + i + 1)
                for c in range(2):
                    if c == 1:
                        pe.wait_ge(im_done, i + 1)
                    for ft in range(FT):
                        last = mm(bank[s][:, M * c:M * c + M], yspec[:, s, c, ft, :], inv[:, c, ft, :],
                                  start=(ft == 0), stop=(ft == FT - 1))
                last.then_inc(eo_done, 1)

            def linear(i, s):
                pe.wait_ge(gelu_done, i + 1)
                if past(i, 2):
                    pe.wait_ge(t_done, i - 1)
                elif i == 0:
                    pe.wait_ge(fwd_out, 4 * FT)
                for t in range(T):
                    o = bank[2 + 2 * s + t // 2][:, 2 * H * (t % 2):2 * H * (t % 2) + 2 * H]
                    mm(o, ones3[:], bias_b[:, 2], start=True, stop=False)
                    last = mm(o, yact[:, s, P * t:P * t + P], w_out[:], start=False, stop=True)
                last.then_inc(z_done, 1)

            def turn_v(i, s):
                pe.wait_ge(v_done, i + 1)
                if past(i, 2):
                    pe.wait_ge(vl_done, i)
                for t in range(T):
                    last = nc.tensor.transpose(turn_bank(i, s)[:, P * t:P * t + P], vbuf[:, s, t, :], ident[:])
                last.then_inc(vt_done, 1)

            def gate_up(i, s, j):
                n = J * i + j
                r = (J * s + j) % 2
                if j == 0:
                    pe.wait_ge(vl_done, i + 1)
                for k, b in ((0, bank[GATE[r]]), (1, bank[UP[j]])):
                    if k == 0 and past(n, 2):
                        pe.wait_ge(silu_done, n - 1)
                    if k == 1 and past(n, J):
                        pe.wait_ge(h_done, n - J + 1)
                    o = slice(HID * k + P * j, HID * k + P * j + P)
                    mm(b[:], wh[:, o], vh[:, s, :], start=True, stop=False)
                    mm(b[:], wh[:, o], vl[:, s, :], start=False, stop=False)
                    last = mm(b[:], wl[:, o], vh[:, s, :], start=False, stop=True)
                last.then_inc(gu_done, 1)

            def down_product(i, s, t, j):
                return mm(out_tile(i, s, t), hb[:, s, j, P * t:P * t + P],
                          w_ffn[:, 2 * HID + H * j:2 * HID + H * j + H], start=(j == 0), stop=(j == J - 1))

            def down(i, s):
                pe.wait_ge(h_done, J * i + J)
                if past(i, 2):
                    pe.wait_ge(w4_done, i - 1)
                else:
                    pe.wait_ge(t_done, B)
                for t in range(T):
                    for j in range(J):
                        last = down_product(i, s, t, j)
                last.then_inc(dn_done, 1)

            pe.wait_ge(inv_in, 16)
            inverse(0, 0)
            forward(3, 3)
            pe.wait_ge(bias_ready, 1)
            pe.wait_ge(w_half, 1)
            pe.wait_ge(setup_p, 4)

            def step(i, s):
                inverse(i + 1, 1 - s)
                linear(i, s)
            step(0, 0)
            step(1, 1)
            unit_steps(pe, 2, B - 2, step)
            pe.wait_ge(ffn_wl, 1)
            step(B - 2, 0)
            turn_v(0, 0)
            linear(B - 1, 1)
            pe.wait_ge(y_done, B)
            gate_up(0, 0, 0)
            turn_v(1, 1)
            pe.wait_ge(t_done, B - 1)
            gate_up(0, 0, 1)
            pe.wait_ge(vl_done, 2)
            gate_up(0, 0, 2)

            def ffn_step(i, s, more=True):
                gate_up(i, s, 0)
                gate_up(i, s, 1)
                if more:
                    turn_v(i + 1, 1 - s)
                down(i - 1, 1 - s)
                gate_up(i, s, 2)
            ffn_step(1, 1)
            unit_steps(pe, 2, B - 2, ffn_step)
            ffn_step(B - 2, 0)
            ffn_step(B - 1, 1, more=False)
            pe.wait_ge(h_done, J * B - 1)
            pe.wait_ge(w4_done, B - 2)
            for t in range(T):
                for j in range(J - 1):
                    down_product(B - 1, 1, t, j)
            pe.wait_ge(h_done, J * B)
            for t in range(T):
                last = down_product(B - 1, 1, t, J - 1)
                if t % 2 == 1:
                    last.then_inc(dn_done, 1)


def kernel(L0_attn_x, L0_attn_log_dt, L0_attn_C_re, L0_attn_C_im, L0_attn_log_A_re, L0_attn_A_im, L0_attn_D,
           L0_attn_W, L0_attn_b, L0_ffn_w_gate, L0_ffn_w_up, L0_ffn_w_down):
    import concourse.bacc as bacc
    from concourse.bass_utils import run_bass_kernel_spmd

    def spread(p):
        q = np.asarray(p).reshape(2, HQ, N2).transpose(0, 2, 1)
        return np.stack([q, q], axis=1).reshape(P, HQ)

    x = np.asarray(L0_attn_x)
    log_dt = np.broadcast_to(np.asarray(L0_attn_log_dt)[:, None], (H, N2))
    arrays = {
        "x": np.concatenate([x[:, M - 1::-1], x[:, M:]], axis=1),
        "ssm": np.concatenate([spread(p) for p in (L0_attn_log_A_re, L0_attn_A_im, L0_attn_C_re, L0_attn_C_im, log_dt)], axis=1),
        "d": np.asarray(L0_attn_D).reshape(2, HQ).T,
        "w": np.asarray(L0_attn_W).T,
        "b": np.broadcast_to(np.asarray(L0_attn_b)[None, :], (3, 2 * H)),
        "ffn": np.concatenate([np.asarray(L0_ffn_w_gate).T, np.asarray(L0_ffn_w_up).T,
                               np.asarray(L0_ffn_w_down).T.reshape(J, P, H).transpose(1, 0, 2).reshape(P, HID)], axis=1),
    }
    arrays.update(shape_constants())
    nc = bacc.Bacc("TRN2", target_bir_lowering=False, num_devices=1)
    arrays = {f"in_{k}": np.ascontiguousarray(v) for k, v in arrays.items()}
    d = {k[3:]: nc.dram_tensor(k, v.shape, mybir.dt.from_np(v.dtype), kind="ExternalInput").ap() for k, v in arrays.items()}
    d["out"] = nc.dram_tensor("out", (B, L, H), F32, kind="ExternalOutput").ap()
    build(nc, d)
    got = run_bass_kernel_spmd(nc, [arrays], core_ids=[0]).results[0]["out"]
    return np.concatenate([got[:, M - 1::-1], got[:, M:]], axis=1)
```
